# Optimizing a Trainium2 kernel written in Bass

```python
import numpy as np
import jax
import jax.numpy as jnp

def _softmax(x, axis=-1):
    return jax.nn.softmax(x, axis=axis)

def _gelu(x):
    return jax.nn.gelu(x, approximate=True)

def _silu(x):
    return jax.nn.silu(x)

def _sigmoid(x):
    return jax.nn.sigmoid(x)

def _layernorm(x, axis=-1, eps=1e-05):
    m = jnp.mean(x, axis=axis, keepdims=True)
    v = jnp.var(x, axis=axis, keepdims=True)
    return (x - m) / jnp.sqrt(v + eps)

def _scatter_add(tgt, idx, src, axis=0):
    return tgt.at[idx].add(src)

def _segment_sum(src, seg, n):
    return jax.ops.segment_sum(src, seg, n)
kernel_name = 'mk_adj_ffn_d1_adj_r2_18bb9a'

def setup_inputs(seed: int=0):
    np.random.seed(seed)
    _w = jnp.asarray

    def _rec_inputs():
        import jax
        import jax.numpy as jnp
        _gk = jax.random.key(seed)
        x = -0.000929 + 1 * jax.random.normal(jax.random.fold_in(_gk, 1), (2048, 128), jnp.float32)
        _w = (1.0 + jnp.arange(2048, dtype=jnp.float32)) ** (-0.5)
        _w = _w / _w.mean()
        _pij = jnp.clip(0.00195312 * _w[:, None] * _w[None, :], 0.0, 1.0)
        _a = jax.random.uniform(jax.random.fold_in(_gk, 2), (2048, 2048)) < _pij
        _a = jnp.logical_or(_a, jnp.eye(2048, dtype=bool))
        _af = _a.astype(jnp.float32)
        _af = _af / jnp.maximum(_af.sum(-1, keepdims=True), 1.0)
        adj = _af
        return (x, adj)
    x, adj = _rec_inputs()

    def _L0_gnn_setup():
        import jax, jax.numpy as jnp
        import numpy as np
        from jax import lax
        D_MODEL = 128
        D_STATE = 16
        D_CONV = 4
        EXPAND = 2
        D_INNER = EXPAND * D_MODEL
        DT_RANK = (D_MODEL + 15) // 16
        N = 2048
        EPS = 1e-05

        def _mamba(h, w_in, conv_w, conv_b, w_xp, w_dt, b_dt, A_log, D_skip, w_out):
            L = h.shape[0]
            xz = h @ w_in
            xc, z = (xz[:, :D_INNER], xz[:, D_INNER:])
            xpad = jnp.pad(xc, ((D_CONV - 1, 0), (0, 0)))
            xconv = sum((xpad[k:k + L] * conv_w[:, k] for k in range(D_CONV))) + conv_b
            u = jax.nn.silu(xconv)
            dbc = u @ w_xp
            dt = jax.nn.softplus(dbc[:, :DT_RANK] @ w_dt + b_dt)
            B = dbc[:, DT_RANK:DT_RANK + D_STATE]
            C = dbc[:, DT_RANK + D_STATE:]
            A = -jnp.exp(A_log)
            dA = jnp.exp(dt[:, :, None] * A[None])
            dBu = dt[:, :, None] * B[:, None, :] * u[:, :, None]

            def step(hst, inp):
                dAt, dBut, Ct = inp
                hst = dAt * hst + dBut
                return (hst, hst @ Ct)
            _, ys = lax.scan(step, jnp.zeros((D_INNER, D_STATE), h.dtype), (dA, dBu, C))
            y = ys + u * D_skip
            y = y * jax.nn.silu(z)
            return y @ w_out
        key = jax.random.key(seed)
        ks = jax.random.split(key, 16)
        x = jax.random.normal(ks[0], (N, D_MODEL), dtype=jnp.float32)
        a = jax.random.uniform(ks[1], (N, N), dtype=jnp.float32)
        adj = a / a.sum(axis=1, keepdims=True)
        s = lambda fi, fo: 1.0 / np.sqrt(fi)
        gcn_w = jax.random.uniform(ks[2], (D_MODEL, D_MODEL), jnp.float32, -s(D_MODEL, 0), s(D_MODEL, 0))
        gcn_b = jnp.zeros((D_MODEL,), jnp.float32)
        ln_g = jnp.ones((D_MODEL,), jnp.float32)
        ln_b = jnp.zeros((D_MODEL,), jnp.float32)
        w_in = jax.random.normal(ks[3], (D_MODEL, 2 * D_INNER), jnp.float32) * s(D_MODEL, 0)
        conv_w = jax.random.normal(ks[4], (D_INNER, D_CONV), jnp.float32) * s(D_CONV, 0)
        conv_b = jnp.zeros((D_INNER,), jnp.float32)
        w_xp = jax.random.normal(ks[5], (D_INNER, DT_RANK + 2 * D_STATE), jnp.float32) * s(D_INNER, 0)
        w_dt = jax.random.normal(ks[6], (DT_RANK, D_INNER), jnp.float32) * s(DT_RANK, 0)
        b_dt = jnp.log(jnp.expm1(jnp.exp(jax.random.uniform(ks[7], (D_INNER,), jnp.float32, np.log(0.001), np.log(0.1)))))
        A_log = jnp.log(jnp.broadcast_to(jnp.arange(1, D_STATE + 1, dtype=jnp.float32), (D_INNER, D_STATE)))
        D_skip = jnp.ones((D_INNER,), jnp.float32)
        w_out = jax.random.normal(ks[8], (D_INNER, D_MODEL), jnp.float32) * s(D_INNER, 0)
        return dict(x=x, adj=adj, gcn_w=gcn_w, gcn_b=gcn_b, ln_g=ln_g, ln_b=ln_b, w_in=w_in, conv_w=conv_w, conv_b=conv_b, w_xp=w_xp, w_dt=w_dt, b_dt=b_dt, A_log=A_log, D_skip=D_skip, w_out=w_out)
    _L0_gnn_all = _L0_gnn_setup()
    _L0_gnn_in = {k: v for k, v in _L0_gnn_all.items() if k in ('gcn_w', 'gcn_b', 'ln_g', 'ln_b', 'w_in', 'conv_w', 'conv_b', 'w_xp', 'w_dt', 'b_dt', 'A_log', 'D_skip', 'w_out')}
    del _L0_gnn_all

    def _L0_ffn_setup():
        import jax, jax.numpy as jnp
        import numpy as np
        N_EXPERTS = 8
        TOP_K = 2
        key = jax.random.key(seed)
        ks = jax.random.split(key, 5)
        B, T, C, E, H = (8, 1024, 128, 8, 341)
        scale = 1.0 / np.sqrt(C)
        return {'x': jax.random.normal(ks[0], (B, T, C), dtype=jnp.float32), 'router_w': jax.random.normal(ks[1], (E, C), dtype=jnp.float32) * scale, 'w1': jax.random.normal(ks[2], (E, H, C), dtype=jnp.float32) * scale, 'w2': jax.random.normal(ks[3], (E, C, H), dtype=jnp.float32) * (1.0 / np.sqrt(H)), 'w3': jax.random.normal(ks[4], (E, H, C), dtype=jnp.float32) * scale}
    _L0_ffn_all = _L0_ffn_setup()
    _L0_ffn_in = {k: v for k, v in _L0_ffn_all.items() if k in ('router_w', 'w1', 'w2', 'w3')}
    del _L0_ffn_all
    return {'x': x, 'adj': adj, 'L0_gnn_gcn_w': _L0_gnn_in['gcn_w'], 'L0_gnn_gcn_b': _L0_gnn_in['gcn_b'], 'L0_gnn_ln_g': _L0_gnn_in['ln_g'], 'L0_gnn_ln_b': _L0_gnn_in['ln_b'], 'L0_gnn_w_in': _L0_gnn_in['w_in'], 'L0_gnn_conv_w': _L0_gnn_in['conv_w'], 'L0_gnn_conv_b': _L0_gnn_in['conv_b'], 'L0_gnn_w_xp': _L0_gnn_in['w_xp'], 'L0_gnn_w_dt': _L0_gnn_in['w_dt'], 'L0_gnn_b_dt': _L0_gnn_in['b_dt'], 'L0_gnn_A_log': _L0_gnn_in['A_log'], 'L0_gnn_D_skip': _L0_gnn_in['D_skip'], 'L0_gnn_w_out': _L0_gnn_in['w_out'], 'L0_ffn_router_w': _L0_ffn_in['router_w'], 'L0_ffn_w1': _L0_ffn_in['w1'], 'L0_ffn_w2': _L0_ffn_in['w2'], 'L0_ffn_w3': _L0_ffn_in['w3']}

def reference(x, adj, L0_gnn_gcn_w, L0_gnn_gcn_b, L0_gnn_ln_g, L0_gnn_ln_b, L0_gnn_w_in, L0_gnn_conv_w, L0_gnn_conv_b, L0_gnn_w_xp, L0_gnn_w_dt, L0_gnn_b_dt, L0_gnn_A_log, L0_gnn_D_skip, L0_gnn_w_out, L0_ffn_router_w, L0_ffn_w1, L0_ffn_w2, L0_ffn_w3):
    import jax
    import jax.numpy as jnp

    def _L0_gnn_ref(x, adj, gcn_w, gcn_b, ln_g, ln_b, w_in, conv_w, conv_b, w_xp, w_dt, b_dt, A_log, D_skip, w_out):
        import jax, jax.numpy as jnp
        import numpy as np
        from jax import lax
        D_MODEL = 128
        D_STATE = 16
        D_CONV = 4
        EXPAND = 2
        D_INNER = EXPAND * D_MODEL
        DT_RANK = (D_MODEL + 15) // 16
        N = 2048
        EPS = 1e-05

        def _mamba(h, w_in, conv_w, conv_b, w_xp, w_dt, b_dt, A_log, D_skip, w_out):
            L = h.shape[0]
            xz = h @ w_in
            xc, z = (xz[:, :D_INNER], xz[:, D_INNER:])
            xpad = jnp.pad(xc, ((D_CONV - 1, 0), (0, 0)))
            xconv = sum((xpad[k:k + L] * conv_w[:, k] for k in range(D_CONV))) + conv_b
            u = jax.nn.silu(xconv)
            dbc = u @ w_xp
            dt = jax.nn.softplus(dbc[:, :DT_RANK] @ w_dt + b_dt)
            B = dbc[:, DT_RANK:DT_RANK + D_STATE]
            C = dbc[:, DT_RANK + D_STATE:]
            A = -jnp.exp(A_log)
            dA = jnp.exp(dt[:, :, None] * A[None])
            dBu = dt[:, :, None] * B[:, None, :] * u[:, :, None]

            def step(hst, inp):
                dAt, dBut, Ct = inp
                hst = dAt * hst + dBut
                return (hst, hst @ Ct)
            _, ys = lax.scan(step, jnp.zeros((D_INNER, D_STATE), h.dtype), (dA, dBu, C))
            y = ys + u * D_skip
            y = y * jax.nn.silu(z)
            return y @ w_out
        h = jax.nn.relu(adj @ x @ gcn_w + gcn_b)
        mu = h.mean(-1, keepdims=True)
        var = h.var(-1, keepdims=True)
        h = (h - mu) * lax.rsqrt(var + EPS) * ln_g + ln_b
        return _mamba(h, w_in, conv_w, conv_b, w_xp, w_dt, b_dt, A_log, D_skip, w_out)

    def _L0_ffn_ref(x, router_w, w1, w2, w3):
        import jax, jax.numpy as jnp
        import numpy as np
        N_EXPERTS = 8
        TOP_K = 2
        B, T, C = x.shape
        flat = x.reshape(-1, C)
        logits = flat @ router_w.T
        probs = jax.nn.softmax(logits, axis=-1)
        topk_probs, topk_idx = jax.lax.top_k(probs, TOP_K)
        topk_probs = topk_probs / (jnp.sum(topk_probs, axis=-1, keepdims=True) + 1e-09)
        onehot = jax.nn.one_hot(topk_idx, N_EXPERTS, dtype=flat.dtype)
        gates = jnp.einsum('nk,nke->ne', topk_probs, onehot)
        h1 = jnp.einsum('nc,ehc->neh', flat, w1)
        h3 = jnp.einsum('nc,ehc->neh', flat, w3)
        h = jax.nn.silu(h1) * h3
        y = jnp.einsum('neh,ech->nec', h, w2)
        out = jnp.einsum('ne,nec->nc', gates, y)
        return out.reshape(B, T, C)
    x = x + _L0_gnn_ref(_layernorm(x, axis=-1), adj, L0_gnn_gcn_w, L0_gnn_gcn_b, L0_gnn_ln_g, L0_gnn_ln_b, L0_gnn_w_in, L0_gnn_conv_w, L0_gnn_conv_b, L0_gnn_w_xp, L0_gnn_w_dt, L0_gnn_b_dt, L0_gnn_A_log, L0_gnn_D_skip, L0_gnn_w_out)
    x = x + _L0_ffn_ref(_layernorm(x, axis=-1)[None], L0_ffn_router_w, L0_ffn_w1, L0_ffn_w2, L0_ffn_w3)[0]
    return x

_drawn_inputs = setup_inputs


def setup_inputs(seed=0):
    import zlib

    import numpy as np

    out = dict(_drawn_inputs(seed))
    spreads = {'L0_gnn_gcn_b': (0.0, 0.1),
     'L0_gnn_ln_g': (1.0, 0.2),
     'L0_gnn_ln_b': (0.0, 0.1),
     'L0_gnn_conv_b': (0.0, 0.1),
     'L0_gnn_D_skip': (1.0, 0.2)}
    factors = {}
    for name, (base, spread) in spreads.items():
        noise = np.random.default_rng([zlib.crc32(name.encode()), seed]).standard_normal(out[name].shape)
        drawn = base * np.exp(spread * noise) if base else spread * noise
        out[name] = jnp.asarray(drawn.astype(out[name].dtype))
    for name, factor in factors.items():
        out[name] = (out[name] * factor).astype(out[name].dtype)
    return out
```

```python
from contextlib import ExitStack

import concourse.bass as bass
from concourse import mybir

F32 = mybir.dt.float32
BF16 = mybir.dt.bfloat16
U32 = mybir.dt.uint32
ALU = mybir.AluOpType
ACT = mybir.ActivationFunctionType

P = 128
L = 2048
D = 128
DI = 256
HALVES = DI // P
NS = 16
RANK = 8
TAPS = 4
E = 8
HID = 341
EPS = 1e-5

T = 512
CHUNKS = L // T
J = T // P
JT = L // P
PIECE = 4
PIECES = JT // PIECE
HT = [128, 128, HID - 256]
STEPS = E * len(HT)
BC0 = 32
PRE = TAPS - 1


STEPS_AFTER = {("xz", 0): 2, ("xp", 0): 1, ("dt", 0): 2, ("gate_y", 0): 1, ("w_out", 0): 2, ("x_turn", 0): 1}
STEPS_AFTER |= {("state", n): 1 for n in range(NS) if n % 3 != 2}
MAMBA = ([("xz", 0), ("xp", 0), ("dt", 0)] + [("state", n) for n in range(NS)] +
         [("gate_y", 0), ("w_out", 0), ("x_turn", 0), ("route", 0)])


def plan(with_ffn):
    steps = list(range(STEPS)) if with_ffn else []
    order = [("ffn_open", 0)] + [("step", steps.pop(0)) for _ in range(2)] if with_ffn else []
    for piece in MAMBA:
        order.append(piece)
        for _ in range(min(STEPS_AFTER.get(piece, 0), len(steps))):
            order.append(("step", steps.pop(0)))
    order += [("step", s) for s in steps]
    if with_ffn:
        order.append(("ffn_close", 0))
    return order + [("gate_x", e) for e in range(E)]


FFN_ALONE = [("ffn_open", 0)] + [("step", s) for s in range(STEPS)] + [("ffn_close", 0)]


def build_kernel(nc, A, out):
    with ExitStack() as ctx:
        def sb(name, shape, dt=F32):
            return ctx.enter_context(nc.sbuf_tensor(name, shape, dt))

        def sem(name):
            return ctx.enter_context(nc.semaphore(name))

        def bank(name):
            return ctx.enter_context(nc.psum_tensor(name, [P, T], F32))

        x_sb = sb("x_sb", [P, JT, D])
        xn1 = sb("xn1", [P, JT, D])
        adj_sb = sb("adj_sb", [P, PIECES, PIECE, T])
        x2 = xn1[:, 0:J, :]
        xn2 = xn1[:, J:2 * J, :]
        gated = xn1[:, 2 * J:4 * J, :].rearrange("p (a j) c -> p a j c", a=2)
        gx = adj_sb[:, 0:2].rearrange("p a b t -> p (a b) t")
        th = adj_sb[:, 2, 0:2, :]
        act1 = adj_sb[:, 2, 2:4, :]
        hid = adj_sb[:, 3, 0:3, :]
        out_sb = adj_sb[:, 3, 3, :]
        gcn_w = sb("gcn_w", [D, D])
        gcn_b = sb("gcn_b", [P, D])
        ln_g = sb("ln_g", [D, 1])
        ln_b = sb("ln_b", [D, 1])
        w_in = sb("w_in", [D, 2 * DI])
        conv_wb = sb("conv_wb", [P, TAPS, DI])
        b_row = conv_wb[:].rearrange("p (a b) d -> p a (b d)", a=2)
        w_tap = sb("w_tap", [D, TAPS, DI])
        conv_b = sb("conv_b", [P, HALVES])
        conv_bh = sb("conv_bh", [P, HALVES])
        w_xp = sb("w_xp", [P, HALVES, P])
        w_dt = sb("w_dt", [RANK, DI])
        b_dt = sb("b_dt", [P, HALVES])
        a_log = sb("a_log", [P, HALVES, NS])
        a_exp = sb("a_exp", [P, HALVES, NS])
        a_neg = sb("a_neg", [P, HALVES, NS])
        d_skip = sb("d_skip", [P, HALVES])
        w_out = sb("w_out", [P, HALVES, D])
        router = sb("router", [D, E])
        w1 = sb("w1", [D, E * HID])
        w3 = sb("w3", [D, E * HID])
        w2 = sb("w2", [P, len(HT), E, D])
        ident = sb("ident", [P, P])
        pick_f = sb("pick_f", [P, 2 * NS])
        pick = sb("pick", [P, 2 * NS, P], BF16)
        iota = sb("iota", [P, E])
        minus_half = sb("minus_half", [P, JT])
        eps_row = sb("eps_row", [P, J])

        stats1 = sb("stats1", [P, JT, 6])
        mv1 = sb("mv1", [P, JT, 2])
        ve1 = sb("ve1", [P, JT])
        rs1 = sb("rs1", [P, JT])
        z_sb = sb("z_sb", [D, T])
        g_pre = sb("g_pre", [P, J, D])
        g_act = g_pre
        statsg = sb("statsg", [P, J, 6])
        mvg = sb("mvg", [P, J, 2])
        veg = sb("veg", [P, J])
        rsg = sb("rsg", [P, J])
        h_nrm = sb("h_nrm", [P, J, D])
        h_t = sb("h_t", [D, PRE + L])

        def x_t(k):
            return h_t[:, bass.ds(k * T, T)]

        xh = sb("xh", [P, HALVES, T])
        xth = sb("xth", [P, HALVES, T])
        zh = sb("zh", [P, HALVES, T])
        zth = sb("zth", [P, HALVES, T])
        u = sb("u", [P, HALVES, T])
        sz = sb("sz", [P, HALVES, T])
        xps = sb("xps", [P, T])
        stack = sb("stack", [P, T], BF16)
        rest1 = sb("rest1", [P, T])
        pre = zh
        ab = xth
        ew = zth
        ln1p = xth
        low = xh
        dt_ = sb("dt_", [P, HALVES, T])
        dtu = sb("dtu", [P, HALVES, T])
        decay = sb("decay", [P, 3, HALVES, T])
        drive = sb("drive", [P, 2, HALVES, T])
        hs = sb("hs", [P, 3, HALVES, T])
        state = sb("state", [P, NS, HALVES])
        prod = sb("prod", [P, 2, HALVES, T])
        yacc = sb("yacc", [P, HALVES, T])
        yg = low
        stats2 = sb("stats2", [P, J, 6])
        mv2 = sb("mv2", [P, J, 2])
        ve2 = sb("ve2", [P, J])
        rs2 = sb("rs2", [P, J])
        x_now = sb("x_now", [D, T])
        logits = sb("logits", [P, J, E])
        top = sb("top", [P, J, 8])
        top_at = sb("top_at", [P, J, 8], U32)
        at_f = sb("at_f", [P, J, 2])
        top_d = sb("top_d", [P, J, 8])
        top_e = sb("top_e", [P, J, 8])
        zsum = sb("zsum", [P, J, 1])
        rz = sb("rz", [P, J, 1])
        prob = sb("prob", [P, J, 2])
        psum2 = sb("psum2", [P, J, 1])
        rp = sb("rp", [P, J, 1])
        gate2 = sb("gate2", [P, J, 2])
        eq0 = sb("eq0", [P, J, E])
        eq1 = sb("eq1", [P, J, E])
        gate = sb("gate", [P, J, E])

        F = [bank(f"F{i}") for i in range(3)]
        H1 = [bank(f"H1_{i}") for i in range(2)]
        H3 = [bank(f"H3_{i}") for i in range(2)]
        OUT = bank("OUT")

        ld_x = sem("ld_x")
        ld_cst = sem("ld_cst")
        ld_adj = [sem(f"ld_adj{i}") for i in range(PIECES)]
        ld_w = sem("ld_w")
        ld_ffn = sem("ld_ffn")
        out_dma = sem("out_dma")
        pe_adj = sem("pe_adj")
        pe_g = sem("pe_g")
        pe_ht = sem("pe_ht")
        act_z = sem("act_z")
        dve_g = sem("dve_g")
        pool_rg = sem("pool_rg")
        dve_hn = sem("dve_hn")
        act_ht = sem("act_ht")
        pool_set = sem("pool_set")
        act_a = sem("act_a")
        dve_prep = sem("dve_prep")
        dve_mv1 = sem("dve_mv1")
        pool_r1 = sem("pool_r1")
        dve_xn1 = sem("dve_xn1")
        dve_ffn_w = sem("dve_ffn_w")
        dve_c = sem("dve_c")
        dve_halved = sem("dve_halved")
        pool_c2 = sem("pool_c2")
        act_c = sem("act_c")
        pool_c = sem("pool_c")
        pe_xz = sem("pe_xz")
        act_xz = sem("act_xz")
        act_xth = sem("act_xth")
        act_zth = sem("act_zth")
        dve_u = sem("dve_u")
        pe_xp = sem("pe_xp")
        act_xp = sem("act_xp")
        dve_stack = sem("dve_stack")
        pe_dt = sem("pe_dt")
        act_pre = sem("act_pre")
        act_ew = sem("act_ew")
        act_ln = sem("act_ln")
        dve_sz = sem("dve_sz")
        dve_dt = sem("dve_dt")
        dve_dtu = sem("dve_dtu")
        pe_B = sem("pe_B")
        pe_C = sem("pe_C")
        act_B = sem("act_B")
        act_keep = sem("act_keep")
        act_decay = sem("act_decay")
        pool_drive = sem("pool_drive")
        dve_scan = sem("dve_scan")
        dve_prod = sem("dve_prod")
        pool_y = sem("pool_y")
        dve_yg = sem("dve_yg")
        pe_wo = sem("pe_wo")
        dve_x2 = sem("dve_x2")
        dve_mv2 = sem("dve_mv2")
        pool_r2 = sem("pool_r2")
        dve_xn2 = sem("dve_xn2")
        pe_xt = sem("pe_xt")
        act_xt = sem("act_xt")
        act_now = sem("act_now")
        pe_rt = sem("pe_rt")
        dve_lg = sem("dve_lg")
        dve_td = sem("dve_td")
        act_te = sem("act_te")
        pe_gt = sem("pe_gt")
        dve_gate = sem("dve_gate")
        pool_gated = sem("pool_gated")
        act_gx = sem("act_gx")
        pe_x2 = sem("pe_x2")
        pe_h1 = sem("pe_h1")
        pe_h3 = sem("pe_h3")
        act_th = sem("act_th")
        dve_a1 = sem("dve_a1")
        dve_hid = sem("dve_hid")
        pe_w2 = sem("pe_w2")
        act_out = sem("act_out")

        def over(ap, shape):
            return ap.broadcast_to(shape)

        small_loads = [
            (ident[:], A["identity"]), (iota[:], A["iota"].partition_broadcast(P)),
            (pick_f[:], A["pick"]),
            (gcn_w[:], A["gcn_w"]), (gcn_b[:], A["gcn_b"].partition_broadcast(P)),
            (ln_g[:], A["ln_g"]), (ln_b[:], A["ln_b"]),
            (conv_b[:], A["conv_b"]), (b_dt[:], A["b_dt"]), (d_skip[:], A["D_skip"]),
            (a_log[:], A["A_log"].rearrange("(h p) n -> p h n", p=P)),
        ]
        w_loads = [
            (w_in[:], A["w_in"]),
            (conv_wb[:], A["conv_w"].partition_broadcast(P)),
            (w_xp[:, :, 0:RANK], A["w_xp"].rearrange("(h p) m -> p h m", p=P)[:, :, 0:RANK]),
        ] + [
            (w_xp[:, :, BC0 + 32 * r:BC0 + 32 * r + 32],
             A["w_xp"].rearrange("(h p) m -> p h m", p=P)[:, :, RANK:RANK + 2 * NS]) for r in range(3)
        ] + [
            (w_dt[:], A["w_dt"]), (w_out[:], A["w_out"].rearrange("(h p) m -> p h m", p=P)),
            (router[:], A["router"]),
        ]
        ffn_loads = [
            (w1[:], A["w1"]), (w3[:], A["w3"]),
        ] + [(w2[0:M, m], A["w2"][m * P:m * P + M]) for m, M in enumerate(HT)]
        block = ctx.enter_context(nc.Block())

        @block.sync
        def _(sp):
            sp.dma_start(x_sb[:], A["x"]).then_inc(ld_x, 16)

            def load_piece(i):
                k, q = divmod(i, PIECES)
                if k >= 1:
                    sp.wait_ge(pe_adj, i - PIECES + 1)
                sp.dma_start(adj_sb[:, q], A["adj"][k, :, q * PIECE:(q + 1) * PIECE, :]).then_inc(ld_adj[q], 16)

            load_piece(0)
            load_piece(1)
            for dst, src in small_loads:
                sp.dma_start(dst, src).then_inc(ld_cst, 16)
            load_piece(2)
            load_piece(3)
            for dst, src in w_loads:
                sp.dma_start(dst, src).then_inc(ld_w, 16)
            for i in range(PIECES, CHUNKS * PIECES):
                load_piece(i)
                if i == 2 * PIECES - 1:
                    for dst, src in ffn_loads:
                        sp.dma_start(dst, src).then_inc(ld_ffn, 16)

            def store(k):
                sp.wait_ge(act_out, k + 1)
                sp.dma_start(out[:, bass.ds(k * T, T)], out_sb).then_inc(out_dma, 16)

            with sp.Fori(0, CHUNKS) as k:
                store(k)
            sp.wait_ge(out_dma, 16 * CHUNKS)

        @block.tensor
        def _(pe):
            def graph(k):
                if k == 0:
                    pe.wait_ge(dve_xn1, 1)
                else:
                    pe.wait_ge(act_z, k)
                for q in range(PIECES):
                    pe.wait_ge(ld_adj[q], 16 * (k + 1))
                    for t in range(PIECE):
                        jt = q * PIECE + t
                        mm = pe.matmul(H1[0][:], xn1[:, jt, :], adj_sb[:, q, t, :], start=(jt == 0), stop=(jt == JT - 1))
                    mm.then_inc(pe_adj, 1)

            def graph_w(k):
                pe.wait_ge(act_z, k + 1)
                if k >= 1:
                    pe.wait_ge(dve_g, k)
                for j in range(J):
                    mm = pe.matmul(H1[1][:, j * P:(j + 1) * P], z_sb[:, j * P:(j + 1) * P], gcn_w[:], start=True, stop=True)
                mm.then_inc(pe_g, 1)

            def graph_turn(k):
                pe.wait_ge(dve_hn, k + 1)
                if k >= 1:
                    pe.wait_ge(act_ht, k)
                for j in range(J):
                    mm = pe.transpose(H3[0][:, j * P:(j + 1) * P], h_nrm[:, j, :], ident[:])
                mm.then_inc(pe_ht, 1)

            def piece(what, i, k, c, first):
                if what == "xz":
                    pe.wait_ge(act_ht, CHUNKS if not first else 1)
                    for m in range(4):
                        b = F[[0, 1, 2, 0][m]]
                        if m < 3 and not first:
                            pe.wait_ge(act_gx, k * E - 2 + m)
                        if m == 3:
                            pe.wait_ge(act_xz, 4 * k + 1)
                        if m < 2:
                            for tap in range(TAPS):
                                mm = pe.matmul(b[:], w_tap[:, tap, m * P:(m + 1) * P], h_t[:, bass.ds(k * T + tap, T)],
                                               start=(tap == 0), stop=(tap == TAPS - 1))
                        else:
                            mm = pe.matmul(b[:], w_in[:, m * P:(m + 1) * P], h_t[:, bass.ds(k * T + PRE, T)], start=True, stop=True)
                        mm.then_inc(pe_xz, 1)
                elif what == "xp":
                    pe.wait_ge(dve_u, k + 1)
                    pe.wait_ge(act_xz, 4 * k + 2)
                    for h in range(HALVES):
                        mm = pe.matmul(F[1][:], w_xp[:, h, :], u[:, h, :], start=(h == 0), stop=(h == HALVES - 1))
                    mm.then_inc(pe_xp, 1)
                elif what == "dt":
                    pe.wait_ge(act_xp, k + 1)
                    pe.wait_ge(act_xz, 4 * k + 4)
                    for h in range(HALVES):
                        b = F[[2, 0][h]]
                        pe.matmul(b[:], w_dt[:, h * P:(h + 1) * P], xps[0:RANK, :], start=True, stop=True).then_inc(pe_dt, 1)
                    pe.wait_ge(dve_stack, k + 1)
                    pe.wait_ge(act_pre, 2 * k + 2)
                    row_of_b(0)
                elif what == "state":
                    if i < NS - 1:
                        pe.wait_ge(act_B, k * NS + i + 1)
                        row_of_b(i + 1)
                    if i >= 2:
                        pe.wait_ge(dve_prod, k * NS + i - 1)
                    pe.matmul(F[i % 2][:], pick[:, NS + i, :], stack[:], start=True, stop=True).then_inc(pe_C, 1)
                elif what == "w_out":
                    pe.wait_ge(dve_yg, k + 1)
                    pe.wait_ge(dve_prod, k * NS + NS)
                    for j in range(J):
                        for h in range(HALVES):
                            mm = pe.matmul(F[0][:, j * P:(j + 1) * P], yg[:, h, j * P:(j + 1) * P], w_out[:, h, :],
                                           start=(h == 0), stop=(h == HALVES - 1))
                    mm.then_inc(pe_wo, 1)
                elif what == "x_turn":
                    pe.wait_ge(dve_xn2, k + 1)
                    for j in range(J):
                        mm = pe.transpose(F[1][:, j * P:(j + 1) * P], xn2[:, j, :], ident[:])
                    mm.then_inc(pe_xt, 1)
                elif what == "route":
                    pe.wait_ge(act_now, k + 1)
                    pe.wait_ge(act_B, k * NS + NS)
                    for j in range(J):
                        mm = pe.matmul(F[2][:, j * E:(j + 1) * E], x_now[:, j * P:(j + 1) * P], router[:], start=True, stop=True)
                    mm.then_inc(pe_rt, 1)
                elif what == "gate_x":
                    pe.wait_ge(pool_gated, k * E + i + 1)
                    if i >= 3:
                        pe.wait_ge(act_gx, k * E + i - 2)
                    elif i == 1:
                        pe.wait_ge(dve_lg, k + 1)
                    for j in range(J):
                        mm = pe.transpose(F[(i + 1) % 3][:, j * P:(j + 1) * P], gated[:, i % 2, j, :], ident[:])
                    mm.then_inc(pe_gt, 1)
                elif what == "ffn_open":
                    if not first:
                        pe.wait_ge(act_out, c)
                    pe.wait_ge(dve_x2, c + 1)
                    for j in range(J):
                        mm = pe.matmul(OUT[:, j * P:(j + 1) * P], x2[:, j, :], ident[:], start=(j == 0), stop=False,
                                       skip_group_check=True)
                    mm.then_inc(pe_x2, 1)
                    pe.wait_ge(act_xt, c + 1)
                elif what == "step":
                    e, m = divmod(i, len(HT))
                    M = HT[m]
                    col = e * HID + m * P
                    if i >= 2:
                        pe.wait_ge(dve_hid, c * STEPS + i - 1)
                    pe.matmul(H1[i % 2][0:M, :], w1[:, col:col + M], x_t(c), start=True, stop=True).then_inc(pe_h1, 1)
                    if m == 0:
                        pe.wait_ge(act_gx, c * E + e + 1)
                    pe.matmul(H3[i % 2][0:M, :], w3[:, col:col + M], gx[:, e, :], start=True, stop=True).then_inc(pe_h3, 1)
                    if i >= 1:
                        down(i - 1, c)
                elif what == "ffn_close":
                    down(STEPS - 1, c)

            def row_of_b(i):
                pe.matmul(F[2][:], pick[:, i, :], stack[:], start=True, stop=True).then_inc(pe_B, 1)

            def down(i, c):
                e, m = divmod(i, len(HT))
                pe.wait_ge(dve_hid, c * STEPS + i + 1)
                pe.matmul(OUT[:], w2[0:HT[m], m, e, :], hid[0:HT[m], i % 3, :], start=False, stop=(i == STEPS - 1),
                          skip_group_check=True).then_inc(pe_w2, 1)

            pe.wait_ge(ld_cst, 16 * len(small_loads))
            graph(0)
            graph_w(0)
            graph(1)
            graph_turn(0)
            pe.wait_ge(ld_w, 16 * len(w_loads))
            pe.wait_ge(dve_prep, 1)
            later = {("state", 1): [(graph_w, 1)], ("state", 2): [(graph, 2)], ("state", 3): [(graph_turn, 1)],
                     ("state", 5): [(graph_w, 2)], ("state", 7): [(graph_turn, 2)], ("state", 8): [(graph, 3)],
                     ("state", 10): [(graph_w, 3)], ("state", 12): [(graph_turn, 3)]}
            for what, i in plan(False):
                piece(what, i, 0, None, True)
                for f, n in later.get((what, i), []):
                    f(n)
            pe.wait_ge(ld_ffn, 16 * len(ffn_loads))
            pe.wait_ge(dve_ffn_w, 1)
            pe.wait_ge(act_ht, CHUNKS)
            for what, i in plan(True):
                piece(what, i, 1, 0, what.startswith("ffn"))
            with pe.Fori(1, CHUNKS - 1) as c:
                for what, i in plan(True):
                    piece(what, i, c + 1, c, False)
            for what, i in FFN_ALONE:
                piece(what, i, None, CHUNKS - 1, False)

        @block.scalar
        def _(act):
            def graph_copy(k):
                act.wait_ge(pe_adj, PIECES * (k + 1))
                if k >= 1:
                    act.wait_ge(pe_g, k)
                act.copy(z_sb[:], H1[0][:]).then_inc(act_z, 1)

            def graph_ht(k):
                act.wait_ge(pe_ht, k + 1)
                act.activation(h_t[:, PRE + k * T:PRE + (k + 1) * T], H3[0][:], ACT.Identity, scale=ln_g[:], bias=ln_b[:])\
                   .then_inc(act_ht, 1)

            def piece(what, i, k, c, first):
                if what == "xz":
                    for m in range(4):
                        act.wait_ge(pe_xz, 4 * k + m + 1)
                        b = F[[0, 1, 2, 0][m]]
                        if m == 0 and not first:
                            act.wait_ge(pe_wo, k)
                        if m < 2:
                            act.activation(xh[:, m, :], b[:], ACT.Identity, bias=conv_bh[:, m:m + 1]).then_inc(act_xz, 1)
                        else:
                            act.copy(zh[:, m - 2, :], b[:]).then_inc(act_xz, 1)
                        if m == 1:
                            act.wait_ge(act_xz, 4 * k + 2)
                            act.activation(xth[:], xh[:], ACT.Tanh).then_inc(act_xth, 1)
                        if m == 3:
                            act.wait_ge(act_xz, 4 * k + 4)
                            act.activation(zth[:], zh[:], ACT.Tanh).then_inc(act_zth, 1)
                elif what == "xp":
                    act.wait_ge(pe_xp, k + 1)
                    act.copy(xps[:], F[1][:]).then_inc(act_xp, 1)
                elif what == "dt":
                    act.wait_ge(dve_sz, k + 1)
                    for h in range(HALVES):
                        act.wait_ge(pe_dt, 2 * k + h + 1)
                        act.activation(pre[:, h, :], F[[2, 0][h]][:], ACT.Identity, bias=b_dt[:, h:h + 1]).then_inc(act_pre, 1)
                    act.wait_ge(act_pre, 2 * k + 2)
                    act.wait_ge(dve_u, k + 1)
                    act.activation(ab[:], pre[:], ACT.Abs).then_inc(act_c, 1)
                    act.wait_ge(act_c, k + 1)
                    act.activation(ew[:], ab[:], ACT.Exp, scale=-1.0).then_inc(act_ew, 1)
                    act.wait_ge(act_ew, k + 1)
                    act.activation(ln1p[:], ew[:], ACT.Ln, bias=1.0).then_inc(act_ln, 1)
                elif what == "state":
                    act.wait_ge(pe_B, k * NS + i + 1)
                    if first and i < 2:
                        pass
                    else:
                        act.wait_ge(pool_drive, k * NS + i - 1)
                    act.copy(b_row[:, i % 2, :], F[2][:]).then_inc(act_B, 1)
                    if i == 0:
                        act.wait_ge(dve_dt, k + 1)
                    if not (first and i < 3):
                        act.wait_ge(dve_scan, 2 * (k * NS + max(i - 2, 0)))
                    for h in range(HALVES):
                        act.activation(decay[:, slot3(i), h, :], dt_[:, h, :], ACT.Exp, scale=a_neg[:, h, i:i + 1]).then_inc(act_decay, 1)
                    if i >= 1:
                        keep(i - 1, k)
                elif what == "gate_y":
                    keep(NS - 1, k)
                elif what == "x_turn":
                    act.wait_ge(pe_xt, k + 1)
                    if not first:
                        act.wait_ge(pe_rt, k)
                    act.copy(x_now[:], F[1][:]).then_inc(act_now, 1)
                    act.copy(x_t(k), F[1][:]).then_inc(act_xt, 1)
                elif what == "route":
                    act.wait_ge(dve_td, k + 1)
                    act.activation(top_e[:], top_d[:], ACT.Exp).then_inc(act_te, 1)
                elif what == "gate_x":
                    act.wait_ge(pe_gt, k * E + i + 1)
                    if first:
                        act.wait_ge(pe_adj, CHUNKS * PIECES)
                    else:
                        act.wait_ge(pe_h3, (k - 1) * STEPS + (i + 1) * len(HT))
                    act.copy(gx[:, i, :], F[(i + 1) % 3][:]).then_inc(act_gx, 1)
                elif what == "step":
                    M = HT[i % len(HT)]
                    act.wait_ge(pe_h1, c * STEPS + i + 1)
                    if not (first and i < 2):
                        act.wait_ge(dve_a1, c * STEPS + i - 1)
                    act.activation(th[0:M, i % 2, :], H1[i % 2][0:M, :], ACT.Tanh).then_inc(act_th, 1)
                elif what == "ffn_close":
                    act.wait_ge(pe_w2, (c + 1) * STEPS)
                    if not first:
                        act.wait_ge(out_dma, 16 * c)
                    act.copy(out_sb, OUT[:]).then_inc(act_out, 1)

            def keep(i, k):
                act.wait_ge(dve_scan, 2 * (k * NS + i + 1))
                act.copy(state[:, i, :], hs[:, slot3(i), :, T - 1]).then_inc(act_keep, 1)

            act.wait_ge(ld_cst, 16 * len(small_loads))
            act.activation(a_exp[:], a_log[:], ACT.Exp).then_inc(act_a, 1)
            graph_copy(0)
            graph_ht(0)
            later = {("state", 0): [(graph_copy, 1)], ("state", 3): [(graph_ht, 1)], ("state", 4): [(graph_copy, 2)],
                     ("state", 7): [(graph_ht, 2)], ("state", 9): [(graph_copy, 3)], ("state", 12): [(graph_ht, 3)]}
            act.wait_ge(dve_prep, 1)
            for what, i in plan(False):
                piece(what, i, 0, None, True)
                for f, n in later.get((what, i), []):
                    f(n)
            for what, i in plan(True):
                piece(what, i, 1, 0, what in ("step", "ffn_close"))
            with act.Fori(1, CHUNKS - 1) as c:
                for what, i in plan(True):
                    piece(what, i, c + 1, c, False)
            for what, i in FFN_ALONE:
                piece(what, i, None, CHUNKS - 1, False)

        @block.vector
        def _(dve):
            def norm_stats(rows, stats, mv, tiles, base, done):
                for j in range(tiles):
                    dve.bn_stats(stats[:, j, :], rows[:, j, :]).then_inc(dve_c, 1)
                for j in range(tiles):
                    dve.wait_ge(dve_c, base + j + 1)
                    dve.bn_aggr(mv[:, j, :], stats[:, j, :]).then_inc(done, 1)

            def norm_rows(dst, rows, mv, rs, tiles, done):
                for j in range(tiles):
                    last = dve.tensor_scalar(dst[:, j, :], rows[:, j, :], mv[:, j, 0:1], rs[:, j:j + 1], ALU.subtract, ALU.mult)
                last.then_inc(done, 1)

            ONCE = 3 + JT
            PER_A = 1 + J
            A_ALL = ONCE + CHUNKS * PER_A

            def graph_rows(k):
                dve.wait_ge(pe_g, k + 1)
                if k >= 1:
                    dve.wait_ge(pe_ht, k)
                dve.tensor_tensor(g_pre[:], H1[1][:].rearrange("p (j c) -> p j c", j=J),
                                  over(gcn_b[:].unsqueeze(1), [P, J, D]), ALU.add).then_inc(dve_g, 1)
                dve.wait_ge(dve_g, k + 1)
                at = ONCE + k * PER_A
                dve.tensor_scalar(g_act[:], g_pre[:], 0.0, None, ALU.max).then_inc(dve_c, 1)
                dve.wait_ge(dve_c, at + 1)
                norm_stats(g_act, statsg, mvg, J, at + 1, dve_mv1)

            def graph_norm(k):
                dve.wait_ge(pool_rg, k + 1)
                norm_rows(h_nrm, g_act, mvg, rsg, J, dve_hn)

            def piece(what, i, k, c, first):
                if what == "xz":
                    dve.wait_ge(act_xth, k + 1)
                    dve.scalar_tensor_tensor(u[:], xth[:], 1.0, xh[:], ALU.add, ALU.mult).then_inc(dve_u, 1)
                    dve.wait_ge(act_zth, k + 1)
                    dve.scalar_tensor_tensor(sz[:], zth[:], 1.0, zh[:], ALU.add, ALU.mult).then_inc(dve_sz, 1)
                elif what == "xp":
                    dve.wait_ge(act_xp, k + 1)
                    if not first:
                        dve.wait_ge(pe_C, k * NS)
                    at = 4 * k
                    dve.tensor_copy(stack[:], xps[:]).then_inc(own_b, 1)
                    dve.wait_ge(own_b, at + 1)
                    dve.tensor_tensor(rest1[64:128, :], xps[64:128, :], stack[64:128, :], ALU.subtract).then_inc(own_b, 1)
                    dve.wait_ge(own_b, at + 2)
                    dve.tensor_copy(stack[64:128, :], rest1[64:128, :]).then_inc(own_b, 1)
                    dve.wait_ge(own_b, at + 3)
                    dve.tensor_tensor(rest1[96:128, :], rest1[96:128, :], stack[96:128, :], ALU.subtract).then_inc(own_b, 1)
                    dve.wait_ge(own_b, at + 4)
                    dve.tensor_copy(stack[96:128, :], rest1[96:128, :]).then_inc(dve_stack, 1)
                elif what == "dt":
                    dve.wait_ge(act_ew, k + 1)
                    at = 3 * k
                    dve.tensor_scalar(low[:], ew[:], 1.0, -1.0, ALU.add, ALU.add).then_inc(own_s, 1)
                    dve.wait_ge(own_s, at + 1)
                    dve.tensor_tensor(low[:], low[:], ew[:], ALU.subtract).then_inc(own_s, 1)
                    dve.wait_ge(own_s, at + 2)
                    dve.wait_ge(act_ln, k + 1)
                    dve.tensor_tensor(low[:], ln1p[:], low[:], ALU.subtract).then_inc(own_s, 1)
                    dve.wait_ge(own_s, at + 3)
                    dve.scalar_tensor_tensor(dt_[:], pre[:], 0.0, low[:], ALU.max, ALU.add).then_inc(dve_dt, 1)
                    dve.wait_ge(dve_dt, k + 1)
                    dve.tensor_tensor(dtu[:], dt_[:], u[:], ALU.mult).then_inc(dve_dtu, 1)
                elif what == "state":
                    if i >= 1:
                        weigh(i - 1, k, first)
                    dve.wait_ge(pool_drive, k * NS + i + 1)
                    for h in range(HALVES):
                        dve.wait_ge(act_decay, 2 * (k * NS + i) + h + 1)
                        start = 0.0 if first else state[:, i, h:h + 1]
                        if h == 0 and not (first and i < 3):
                            dve.wait_ge(act_keep, k * NS + max(i - 2, 0))
                            dve.wait_ge(dve_prod, k * NS + max(i - 2, 0))
                        dve.tensor_tensor_scan(hs[:, slot3(i), h, :], decay[:, slot3(i), h, :], drive[:, i % 2, h, :], start,
                                               ALU.mult, ALU.add).then_inc(dve_scan, 1)
                elif what == "gate_y":
                    weigh(NS - 1, k, first)
                    dve.wait_ge(pool_y, (k + 1) * (NS - 1))
                    for h in range(HALVES):
                        dve.scalar_tensor_tensor(yacc[:, h, :], u[:, h, :], d_skip[:, h:h + 1], yacc[:, h, :], ALU.mult, ALU.add)\
                           .then_inc(own_y, 1)
                    dve.wait_ge(own_y, 2 * k + 2)
                    dve.tensor_tensor(yg[:], yacc[:], sz[:], ALU.mult).then_inc(dve_yg, 1)
                elif what == "w_out":
                    dve.wait_ge(pe_wo, k + 1)
                    if not first:
                        dve.wait_ge(pe_x2, k)
                    dve.tensor_tensor(x2, F[0][:].rearrange("p (j c) -> p j c", j=J),
                                      x_sb[:, bass.ds(k * J, J), :], ALU.add).then_inc(dve_x2, 1)
                    dve.wait_ge(dve_x2, k + 1)
                    for j in range(J):
                        dve.bn_stats(stats2[:, j, :], x2[:, j, :]).then_inc(own_n, 1)
                    for j in range(J):
                        dve.wait_ge(ld_x, 16)
                        dve.wait_ge(own_n, J * k + j + 1)
                        dve.bn_aggr(mv2[:, j, :], stats2[:, j, :]).then_inc(dve_mv2, 1)
                elif what == "x_turn":
                    dve.wait_ge(pool_r2, k + 1)
                    norm_rows(xn2, x2, mv2, rs2, J, dve_xn2)
                elif what == "route":
                    route(k)
                elif what == "step":
                    M = HT[i % len(HT)]
                    dve.wait_ge(act_th, c * STEPS + i + 1)
                    dve.scalar_tensor_tensor(act1[0:M, i % 2, :], th[0:M, i % 2, :], 1.0, H1[i % 2][0:M, :], ALU.add, ALU.mult)\
                       .then_inc(dve_a1, 1)
                    dve.wait_ge(dve_a1, c * STEPS + i + 1)
                    dve.wait_ge(pe_h3, c * STEPS + i + 1)
                    if not (first and i < 3):
                        dve.wait_ge(pe_w2, c * STEPS + i - 2)
                    dve.tensor_tensor(hid[0:M, i % 3, :], act1[0:M, i % 2, :], H3[i % 2][0:M, :], ALU.mult).then_inc(dve_hid, 1)

            def weigh(i, k, first):
                dve.wait_ge(pe_C, k * NS + i + 1)
                dve.wait_ge(dve_scan, 2 * (k * NS + i + 1))
                if not (first and i < 3):
                    dve.wait_ge(pool_y, k * (NS - 1) + max(i - 2, 0))
                dst = yacc[:] if i == 0 else prod[:, i % 2]
                dve.tensor_tensor(dst, hs[:, slot3(i)], over(F[i % 2][:].unsqueeze(1), [P, HALVES, T]), ALU.mult).then_inc(dve_prod, 1)

            def route(k):
                n = [0]

                def own(ins):
                    n[0] += 1
                    ins.then_inc(own_r, 1)
                    dve.wait_ge(own_r, ROUTE * k + n[0])

                dve.wait_ge(pe_rt, k + 1)
                dve.tensor_copy(logits[:], F[2][:, 0:J * E].rearrange("p (j e) -> p j e", j=J)).then_inc(dve_lg, 1)
                for j in range(J):
                    dve.wait_ge(ld_x, 16)
                    dve.wait_ge(dve_lg, k + 1)
                    dve.max(top[:, j, :], logits[:, j, :]).then_inc(own_r, 1)
                dve.wait_ge(own_r, ROUTE * k + J)
                dve.tensor_tensor(top_d[:], top[:], over(top[:, :, 0:1], [P, J, 8]), ALU.subtract).then_inc(dve_td, 1)
                for j in range(J):
                    dve.max_index(top_at[:, j, :], top[:, j, :], logits[:, j, :]).then_inc(own_r, 1)
                n[0] = 2 * J
                dve.wait_ge(own_r, ROUTE * k + 2 * J)
                own(dve.tensor_copy(at_f[:], top_at[:, :, 0:2]))
                own(dve.tensor_tensor(eq0[:], over(iota[:].unsqueeze(1), [P, J, E]), over(at_f[:, :, 0:1], [P, J, E]), ALU.is_equal))
                own(dve.tensor_tensor(eq1[:], over(iota[:].unsqueeze(1), [P, J, E]), over(at_f[:, :, 1:2], [P, J, E]), ALU.is_equal))
                dve.wait_ge(act_te, k + 1)
                own(dve.tensor_reduce(zsum[:], top_e[:], mybir.AxisListType.X, ALU.add))
                own(dve.reciprocal(rz[:], zsum[:]))
                own(dve.tensor_tensor(prob[:], top_e[:, :, 0:2], over(rz[:], [P, J, 2]), ALU.mult))
                own(dve.tensor_tensor(psum2[:], prob[:, :, 0:1], prob[:, :, 1:2], ALU.add))
                own(dve.tensor_scalar(psum2[:], psum2[:], 1e-9, None, ALU.add))
                own(dve.reciprocal(rp[:], psum2[:]))
                own(dve.tensor_tensor(gate2[:], prob[:], over(rp[:], [P, J, 2]), ALU.mult))
                own(dve.tensor_tensor(eq0[:], eq0[:], over(gate2[:, :, 0:1], [P, J, E]), ALU.mult))
                own(dve.tensor_tensor(eq1[:], eq1[:], over(gate2[:, :, 1:2], [P, J, E]), ALU.mult))
                dve.tensor_tensor(gate[:], eq0[:], eq1[:], ALU.add).then_inc(dve_gate, 1)
                assert n[0] == ROUTE

            own_b, own_s, own_y, own_n, own_r = sem("own_b"), sem("own_s"), sem("own_y"), sem("own_n"), sem("own_r")
            ROUTE = 20

            dve.wait_ge(ld_x, 16)
            norm_stats(x_sb, stats1, mv1, JT, 0, dve_mv1)
            dve.wait_ge(pool_r1, 1)
            norm_rows(xn1, x_sb, mv1, rs1, JT, dve_xn1)
            dve.wait_ge(ld_cst, 16 * len(small_loads))
            dve.wait_ge(act_a, 1)
            dve.tensor_scalar(a_neg[:], a_exp[:], -1.0, None, ALU.mult).then_inc(dve_c, 1)
            dve.tensor_scalar(conv_bh[:], conv_b[:], 0.5, None, ALU.mult).then_inc(dve_c, 1)
            dve.wait_ge(ld_w, 16 * len(w_loads))
            dve.scalar_tensor_tensor(w_tap[:], conv_wb[:], 0.5, over(w_in[:, 0:DI].unsqueeze(1), [P, TAPS, DI]), ALU.mult, ALU.mult)\
               .then_inc(dve_c, 1)
            dve.tensor_scalar(w_in[:, DI:2 * DI], w_in[:, DI:2 * DI], 0.5, None, ALU.mult).then_inc(dve_halved, 1)
            dve.wait_ge(dve_c, ONCE)
            dve.wait_ge(dve_halved, 1)
            dve.wait_ge(pool_set, 6)
            dve.engine_nop().then_inc(dve_prep, 1)
            graph_rows(0)
            graph_norm(0)
            later = {("state", 2): [(graph_rows, 1)], ("state", 3): [(graph_norm, 1)],
                     ("state", 6): [(graph_rows, 2)], ("state", 7): [(graph_norm, 2)],
                     ("state", 11): [(graph_rows, 3)], ("state", 12): [(graph_norm, 3)]}
            for what, i in plan(False):
                piece(what, i, 0, None, True)
                for f, n in later.get((what, i), []):
                    f(n)
            dve.wait_ge(ld_ffn, 16 * len(ffn_loads))
            dve.tensor_scalar(w1[:], w1[:], 0.5, None, ALU.mult).then_inc(dve_ffn_w, 1)
            for what, i in plan(True):
                piece(what, i, 1, 0, what == "step")
            with dve.Fori(1, CHUNKS - 1) as c:
                for what, i in plan(True):
                    piece(what, i, c + 1, c, False)
            for what, i in FFN_ALONE:
                piece(what, i, None, CHUNKS - 1, False)

        @block.gpsimd
        def _(pool):
            def rstd(mv, ve, rs, own_at, done):
                pool.tensor_scalar(ve[:], mv[:, :, 1], EPS, None, ALU.add).then_inc(pool_c, 1)
                pool.wait_ge(pool_c, own_at + 1)
                n = ve.shape[1]
                pool.tensor_tensor(rs[:], ve[:], minus_half[:, 0:n], ALU.pow).then_inc(done, 1)

            def graph_r(k):
                pool.wait_ge(dve_mv1, JT + (k + 1) * J)
                rstd(mvg, veg, rsg, 1 + k, pool_rg)

            def piece(what, i, k, c, first):
                if what == "state":
                    if i == 0:
                        pool.wait_ge(dve_dtu, k + 1)
                    pool.wait_ge(act_B, k * NS + i + 1)
                    if not (first and i < 2):
                        pool.wait_ge(dve_scan, 2 * (k * NS + i - 1))
                    pool.tensor_tensor(drive[:, i % 2], dtu[:], over(b_row[:, i % 2, :].unsqueeze(1), [P, HALVES, T]), ALU.mult)\
                        .then_inc(pool_drive, 1)
                    if i >= 3:
                        add(i - 2, k, first)
                elif what == "gate_y":
                    add(NS - 2, k, first)
                    add(NS - 1, k, first)
                elif what == "w_out":
                    pool.wait_ge(dve_mv2, (k + 1) * J)
                    pool.tensor_tensor(ve2[:], mv2[:, :, 1], eps_row[:], ALU.add).then_inc(pool_c2, 1)
                    pool.wait_ge(pool_c2, k + 1)
                    pool.tensor_tensor(rs2[:], ve2[:], minus_half[:, 0:J], ALU.pow).then_inc(pool_r2, 1)
                elif what == "gate_x":
                    if i == 0:
                        pool.wait_ge(dve_gate, k + 1)
                    if not (first and i < 2):
                        pool.wait_ge(pe_gt, k * E + i - 1)
                    pool.tensor_tensor(gated[:, i % 2], xn2, over(gate[:, :, i:i + 1], [P, J, D]), ALU.mult)\
                        .then_inc(pool_gated, 1)

            def add(i, k, first):
                pool.wait_ge(dve_prod, k * NS + i + 1)
                if i >= 2:
                    pool.wait_ge(pool_y, k * (NS - 1) + i - 1)
                pool.tensor_tensor(yacc[:], yacc[:], prod[:, i % 2], ALU.add).then_inc(pool_y, 1)

            pool.memset(minus_half[:], -0.5).then_inc(pool_set, 1)
            pool.memset(w_xp[:, :, RANK:BC0], 0.0).then_inc(pool_set, 1)
            pool.memset(h_t[:, 0:PRE], 0.0).then_inc(pool_set, 1)
            pool.memset(eps_row[:], EPS).then_inc(pool_set, 1)
            pool.wait_ge(pool_set, 4)
            pool.wait_ge(dve_mv1, JT)
            rstd(mv1, ve1, rs1, 0, pool_r1)
            pool.wait_ge(ld_cst, 16 * len(small_loads))
            pool.tensor_copy(pick[:, 0:NS], over(pick_f[:, 0:NS].unsqueeze(2), [P, NS, P])).then_inc(pool_set, 1)
            pool.tensor_copy(pick[:, NS:2 * NS], over(pick_f[:, NS:2 * NS].unsqueeze(2), [P, NS, P])).then_inc(pool_set, 1)
            graph_r(0)
            later = {("state", 2): [(graph_r, 1)], ("state", 6): [(graph_r, 2)], ("state", 11): [(graph_r, 3)]}
            for what, i in plan(False):
                piece(what, i, 0, None, True)
                for f, n in later.get((what, i), []):
                    f(n)
            with pool.Fori(1, CHUNKS) as k:
                for what, i in plan(False):
                    piece(what, i, k, None, False)


def slot3(i):
    return i % 3


def kernel(x, adj, L0_gnn_gcn_w, L0_gnn_gcn_b, L0_gnn_ln_g, L0_gnn_ln_b, L0_gnn_w_in, L0_gnn_conv_w,
           L0_gnn_conv_b, L0_gnn_w_xp, L0_gnn_w_dt, L0_gnn_b_dt, L0_gnn_A_log, L0_gnn_D_skip, L0_gnn_w_out,
           L0_ffn_router_w, L0_ffn_w1, L0_ffn_w2, L0_ffn_w3):
    import numpy as np
    import concourse.bacc as bacc
    from concourse.bass_utils import run_bass_kernel_spmd

    def tiles(a):
        a = np.asarray(a)
        return a.reshape(-1, P, a.shape[1]).transpose(1, 0, 2)

    def channels(v):
        return np.asarray(v).reshape(HALVES, P).T

    pick = np.zeros((P, 2 * NS), np.float32)
    for r in range(3):
        pick[BC0 + 32 * r:BC0 + 32 * r + 32, :] = np.eye(2 * NS, dtype=np.float32)
    arrays = {
        "x": tiles(x),
        "adj": np.asarray(adj).reshape(CHUNKS, T, JT, P).transpose(0, 3, 2, 1),
        "gcn_w": L0_gnn_gcn_w, "gcn_b": L0_gnn_gcn_b,
        "ln_g": np.asarray(L0_gnn_ln_g).reshape(D, 1), "ln_b": np.asarray(L0_gnn_ln_b).reshape(D, 1),
        "w_in": L0_gnn_w_in, "conv_w": np.asarray(L0_gnn_conv_w).T, "conv_b": channels(L0_gnn_conv_b),
        "w_xp": L0_gnn_w_xp, "w_dt": L0_gnn_w_dt, "b_dt": channels(L0_gnn_b_dt),
        "A_log": L0_gnn_A_log, "D_skip": channels(L0_gnn_D_skip), "w_out": L0_gnn_w_out,
        "router": np.asarray(L0_ffn_router_w).T,
        "w1": np.asarray(L0_ffn_w1).reshape(E * HID, D).T,
        "w3": np.asarray(L0_ffn_w3).reshape(E * HID, D).T,
        "w2": np.asarray(L0_ffn_w2).transpose(2, 0, 1),
        "identity": np.eye(P, dtype=np.float32),
        "pick": pick,
        "iota": np.arange(E, dtype=np.float32),
    }
    nc = bacc.Bacc("TRN2", target_bir_lowering=False, num_devices=1)
    sent, args = {}, {}
    for name, a in arrays.items():
        a = np.ascontiguousarray(a)
        sent[f"in_{name}"] = a
        args[name] = nc.dram_tensor(f"in_{name}", a.shape, mybir.dt.from_np(a.dtype), kind="ExternalInput").ap()
    out = nc.dram_tensor("out_t", (D, L), F32, kind="ExternalOutput").ap()
    build_kernel(nc, args, out)
    result = run_bass_kernel_spmd(nc, [sent], core_ids=[0])
    return np.ascontiguousarray(result.results[0]["out_t"].T)
```

```python
from contextlib import ExitStack

import concourse.bass as bass
from concourse import mybir

F32 = mybir.dt.float32
BF16 = mybir.dt.bfloat16
U32 = mybir.dt.uint32
ALU = mybir.AluOpType
ACT = mybir.ActivationFunctionType

P = 128
L = 2048
D = 128
DI = 256
HALVES = DI // P
NS = 16
RANK = 8
TAPS = 4
E = 8
HID = 341
EPS = 1e-5

T = 512
CHUNKS = L // T
J = T // P
JT = L // P
PIECE = 4
PIECES = JT // PIECE
HT = [128, 128, HID - 256]
STEPS = E * len(HT)
BC0 = 32
PRE = TAPS - 1


OWN_ALONE = (2, 4, 6, 8, 10, 12, 13, 14, 15)
OWN_BESIDE = (13, 14, 15)


def own_states(k):
    return OWN_ALONE if isinstance(k, int) and k == 0 else OWN_BESIDE


def shared(n_own):
    return NS - n_own - 1


def adds_before(k):
    if isinstance(k, int) and k == 0:
        return 0
    return shared(len(OWN_ALONE)) + (k - 1) * shared(len(OWN_BESIDE))


def states(k, c=None, gates_of=None):
    order = []
    gates = [("gate_x", e, gates_of) for e in range(E)] if gates_of is not None else []
    steps = [("step", s, c) for s in range(STEPS)] if c is not None else []
    for n in range(NS):
        order += gates[:2]
        del gates[:2]
        order.append(("state", n, k))
        if steps and n == 3:
            order.append(("ffn_open", 0, c))
        if n >= 3:
            m = -(-len(steps) // (NS - n))
            order += steps[:m]
            del steps[:m]
    if c is not None:
        order.append(("ffn_close", 0, c))
    return order


def seam(k, m):
    woven = [("gate_y", k), ("x_half", m), ("w_out", k), ("z_half", m), ("x_turn", k), ("xp", m), ("route", k), ("dt", m)]
    return [(what, 0, at) for what, at in woven if at is not None]


def ffn_alone(c):
    return ([("gate_x", e, c) for e in range(E)] + [("ffn_open", 0, c)] + [("step", s, c) for s in range(STEPS)] +
            [("ffn_close", 0, c)])


def build_kernel(nc, A, out):
    with ExitStack() as ctx:
        def sb(name, shape, dt=F32):
            return ctx.enter_context(nc.sbuf_tensor(name, shape, dt))

        def sem(name):
            return ctx.enter_context(nc.semaphore(name))

        def bank(name):
            return ctx.enter_context(nc.psum_tensor(name, [P, T], F32))

        x_sb = sb("x_sb", [P, JT, D])
        xn1 = sb("xn1", [P, JT, D])
        adj_sb = sb("adj_sb", [P, PIECES, PIECE, T])
        x2 = xn1[:, 0:J, :]
        xn2 = xn1[:, J:2 * J, :]
        gated = xn1[:, 2 * J:4 * J, :].rearrange("p (a j) c -> p a j c", a=2)
        gx = adj_sb[:, 0:2].rearrange("p a b t -> p (a b) t")
        th = adj_sb[:, 2, 0:4, :]
        hid = adj_sb[:, 3, 0:3, :]
        out_sb = adj_sb[:, 3, 3, :]
        gcn_w = sb("gcn_w", [D, D])
        gcn_b = sb("gcn_b", [P, D])
        ln_g = sb("ln_g", [D, 1])
        ln_b = sb("ln_b", [D, 1])
        w_in = sb("w_in", [D, 2 * DI])
        conv_wb = sb("conv_wb", [P, TAPS, DI])
        b_row = conv_wb[:].rearrange("p (a b) d -> p a (b d)", a=2)
        w_tap = sb("w_tap", [D, TAPS, DI])
        conv_b = sb("conv_b", [P, HALVES])
        conv_bh = sb("conv_bh", [P, HALVES])
        w_xp = sb("w_xp", [P, HALVES, P])
        w_dt = sb("w_dt", [RANK, DI])
        b_dt = sb("b_dt", [P, HALVES])
        a_log = sb("a_log", [P, HALVES, NS])
        a_exp = sb("a_exp", [P, HALVES, NS])
        a_neg = sb("a_neg", [P, HALVES, NS])
        d_skip = sb("d_skip", [P, HALVES])
        w_out = sb("w_out", [P, HALVES, D])
        router = sb("router", [D, E])
        w1 = sb("w1", [D, E * HID])
        w3 = sb("w3", [D, E * HID])
        w2 = sb("w2", [P, len(HT), E, D])
        ident = sb("ident", [P, P])
        pick_f = sb("pick_f", [P, 2 * NS])
        pick = sb("pick", [P, 2 * NS, P], BF16)
        iota = sb("iota", [P, E])
        minus_half = sb("minus_half", [P, JT])
        eps_row = sb("eps_row", [P, J])
        one = sb("one", [P, HALVES])

        stats1 = sb("stats1", [P, JT, 6])
        mv1 = sb("mv1", [P, JT, 2])
        ve1 = sb("ve1", [P, JT])
        rs1 = sb("rs1", [P, JT])
        z_sb = sb("z_sb", [D, T])
        g_pre = sb("g_pre", [P, J, D])
        g_act = g_pre
        statsg = sb("statsg", [P, J, 6])
        mvg = sb("mvg", [P, J, 2])
        veg = sb("veg", [P, J])
        rsg = sb("rsg", [P, J])
        h_nrm = sb("h_nrm", [P, J, D])
        h_t = sb("h_t", [D, PRE + L])

        def x_t(k):
            return h_t[:, bass.ds(k * T, T)]

        xh = sb("xh", [P, HALVES, T])
        xth = sb("xth", [P, HALVES, T])
        zh = sb("zh", [P, HALVES, T])
        zth = sb("zth", [P, HALVES, T])
        u = sb("u", [P, HALVES, T])
        sz = sb("sz", [P, HALVES, T])
        xps = sb("xps", [P, T])
        stack = sb("stack", [P, T], BF16)
        pre = zh
        ab = xth
        ew = zth
        ln1p = xth
        low = xh
        dt_ = sb("dt_", [P, HALVES, T])
        rest = dt_[:, 0, :]
        dtu = sb("dtu", [P, HALVES, T])
        decay = sb("decay", [P, 3, HALVES, T])
        drive = sb("drive", [P, 2, HALVES, T])
        hs = sb("hs", [P, 3, HALVES, T])
        state = sb("state", [P, NS, HALVES])
        prod = sb("prod", [P, 2, HALVES, T])
        yacc = sb("yacc", [P, HALVES, T])
        yg = yacc
        yown = sb("yown", [P, HALVES, T])
        ptmp = sb("ptmp", [P, HALVES, T])
        stats2 = sb("stats2", [P, J, 6])
        mv2 = sb("mv2", [P, J, 2])
        ve2 = sb("ve2", [P, J])
        rs2 = sb("rs2", [P, J])
        x_now = z_sb
        logits = sb("logits", [P, J, E])
        top = sb("top", [P, J, 8])
        top_at = sb("top_at", [P, J, 8], U32)
        at_f = sb("at_f", [P, J, 2])
        top_d = sb("top_d", [P, J, 8])
        top_e = sb("top_e", [P, J, 8])
        zsum = sb("zsum", [P, J, 1])
        rz = sb("rz", [P, J, 1])
        prob = sb("prob", [P, J, 2])
        psum2 = sb("psum2", [P, J, 1])
        rp = sb("rp", [P, J, 1])
        gate2 = sb("gate2", [P, J, 2])
        eq0, eq1, gate = [stats1[:].rearrange("p t s -> p (t s)")[:, i * J * E:(i + 1) * J * E].rearrange("p (j e) -> p j e", j=J)
                          for i in range(3)]

        F = [bank(f"F{i}") for i in range(3)]
        H1 = [bank(f"H1_{i}") for i in range(2)]
        H3 = [bank(f"H3_{i}") for i in range(2)]
        OUT = bank("OUT")

        ld_x = sem("ld_x")
        ld_cst = sem("ld_cst")
        ld_adj = [sem(f"ld_adj{i}") for i in range(PIECES)]
        ld_w = sem("ld_w")
        ld_ffn = sem("ld_ffn")
        out_dma = sem("out_dma")
        pe_adj = sem("pe_adj")
        pe_g = sem("pe_g")
        pe_ht = sem("pe_ht")
        act_z = sem("act_z")
        dve_g = sem("dve_g")
        pool_rg = sem("pool_rg")
        dve_hn = sem("dve_hn")
        act_ht = sem("act_ht")
        pool_set = sem("pool_set")
        act_a = sem("act_a")
        dve_prep = sem("dve_prep")
        dve_mv1 = sem("dve_mv1")
        pool_r1 = sem("pool_r1")
        dve_xn1 = sem("dve_xn1")
        dve_ffn_w = sem("dve_ffn_w")
        dve_c = sem("dve_c")
        dve_halved = sem("dve_halved")
        pool_c2 = sem("pool_c2")
        act_c = sem("act_c")
        pool_c = sem("pool_c")
        pe_xz = sem("pe_xz")
        act_xz = sem("act_xz")
        act_xth = sem("act_xth")
        act_zth = sem("act_zth")
        dve_u = sem("dve_u")
        pool_stack = sem("pool_stack")
        pool_sz = sem("pool_sz")
        pe_xp = sem("pe_xp")
        act_xp = sem("act_xp")
        pe_dt = sem("pe_dt")
        act_pre = sem("act_pre")
        act_ew = sem("act_ew")
        act_ln = sem("act_ln")
        dve_dt = sem("dve_dt")
        dve_dtu = sem("dve_dtu")
        pe_B = sem("pe_B")
        pe_C = sem("pe_C")
        act_B = sem("act_B")
        act_keep = sem("act_keep")
        act_decay = sem("act_decay")
        pool_drive = sem("pool_drive")
        dve_scan = sem("dve_scan")
        dve_prod = sem("dve_prod")
        pool_y = sem("pool_y")
        dve_yg = sem("dve_yg")
        pe_wo = sem("pe_wo")
        dve_x2 = sem("dve_x2")
        dve_mv2 = sem("dve_mv2")
        pool_r2 = sem("pool_r2")
        dve_xn2 = sem("dve_xn2")
        pe_xt = sem("pe_xt")
        act_xt = sem("act_xt")
        act_now = sem("act_now")
        pe_rt = sem("pe_rt")
        dve_lg = sem("dve_lg")
        dve_td = sem("dve_td")
        act_te = sem("act_te")
        pe_gt = sem("pe_gt")
        dve_gate = sem("dve_gate")
        pool_gated = sem("pool_gated")
        act_gx = sem("act_gx")
        pe_x2 = sem("pe_x2")
        pe_h1 = sem("pe_h1")
        pe_h3 = sem("pe_h3")
        act_th = sem("act_th")
        dve_a1 = sem("dve_a1")
        dve_hid = sem("dve_hid")
        pe_w2 = sem("pe_w2")
        act_out = sem("act_out")

        def over(ap, shape):
            return ap.broadcast_to(shape)

        small_loads = [
            (ident[:], A["identity"]), (iota[:], A["iota"].partition_broadcast(P)),
            (pick_f[:], A["pick"]),
            (gcn_w[:], A["gcn_w"]), (gcn_b[:], A["gcn_b"].partition_broadcast(P)),
            (ln_g[:], A["ln_g"]), (ln_b[:], A["ln_b"]),
            (conv_b[:], A["conv_b"]), (b_dt[:], A["b_dt"]), (d_skip[:], A["D_skip"]),
            (a_log[:], A["A_log"].rearrange("(h p) n -> p h n", p=P)),
        ]
        w_loads = [
            (w_in[:], A["w_in"]),
            (conv_wb[:], A["conv_w"].partition_broadcast(P)),
            (w_xp[:, :, 0:RANK], A["w_xp"].rearrange("(h p) m -> p h m", p=P)[:, :, 0:RANK]),
        ] + [
            (w_xp[:, :, BC0 + 32 * r:BC0 + 32 * r + 32],
             A["w_xp"].rearrange("(h p) m -> p h m", p=P)[:, :, RANK:RANK + 2 * NS]) for r in range(3)
        ] + [
            (w_dt[:], A["w_dt"]), (w_out[:], A["w_out"].rearrange("(h p) m -> p h m", p=P)),
            (router[:], A["router"]),
        ]
        ffn_loads = [
            (w1[:], A["w1"]), (w3[:], A["w3"]),
        ] + [(w2[0:M, m], A["w2"][m * P:m * P + M]) for m, M in enumerate(HT)]
        block = ctx.enter_context(nc.Block())

        @block.sync
        def _(sp):
            sp.dma_start(x_sb[:], A["x"]).then_inc(ld_x, 16)

            def load_piece(i):
                k, q = divmod(i, PIECES)
                if k >= 1:
                    sp.wait_ge(pe_adj, i - PIECES + 1)
                sp.dma_start(adj_sb[:, q], A["adj"][k, :, q * PIECE:(q + 1) * PIECE, :]).then_inc(ld_adj[q], 16)

            load_piece(0)
            load_piece(1)
            for dst, src in small_loads:
                sp.dma_start(dst, src).then_inc(ld_cst, 16)
            load_piece(2)
            load_piece(3)
            for dst, src in w_loads:
                sp.dma_start(dst, src).then_inc(ld_w, 16)
            for i in range(PIECES, CHUNKS * PIECES):
                load_piece(i)
                if i == 2 * PIECES - 1:
                    for dst, src in ffn_loads:
                        sp.dma_start(dst, src).then_inc(ld_ffn, 16)

            def store(k):
                sp.wait_ge(act_out, k + 1)
                sp.dma_start(out[:, bass.ds(k * T, T)], out_sb).then_inc(out_dma, 16)

            with sp.Fori(0, CHUNKS) as k:
                store(k)
            sp.wait_ge(out_dma, 16 * CHUNKS)

        @block.tensor
        def _(pe):
            def graph(k, pieces=range(PIECES)):
                if k >= 1:
                    pe.wait_ge(act_z, k)
                for q in pieces:
                    pe.wait_ge(ld_adj[q], 16 * (k + 1))
                    for t in range(PIECE):
                        jt = q * PIECE + t
                        mm = pe.matmul(OUT[:], xn1[:, jt, :], adj_sb[:, q, t, :], start=(jt == 0), stop=(jt == JT - 1))
                    mm.then_inc(pe_adj, 1)

            def graph_w(k):
                pe.wait_ge(act_z, k + 1)
                if k >= 1:
                    pe.wait_ge(dve_g, k)
                for j in range(J):
                    mm = pe.matmul(H3[0][:, j * P:(j + 1) * P], z_sb[:, j * P:(j + 1) * P], gcn_w[:], start=True, stop=True)
                mm.then_inc(pe_g, 1)

            def graph_turn(k):
                pe.wait_ge(dve_hn, k + 1)
                if k >= 1:
                    pe.wait_ge(act_ht, k)
                for j in range(J):
                    mm = pe.transpose(H3[1][:, j * P:(j + 1) * P], h_nrm[:, j, :], ident[:])
                mm.then_inc(pe_ht, 1)

            def piece(what, i, k):
                later = not (isinstance(k, int) and k == 0)
                if what == "x_half":
                    if later:
                        pe.wait_ge(act_ht, CHUNKS)
                        pe.wait_ge(act_B, k * NS)
                    else:
                        pe.wait_ge(act_ht, 1)
                    for h in range(HALVES):
                        for tap in range(TAPS):
                            mm = pe.matmul([F[2], H1[0]][h][:], w_tap[:, tap, h * P:(h + 1) * P], h_t[:, bass.ds(k * T + tap, T)],
                                           start=(tap == 0), stop=(tap == TAPS - 1))
                        mm.then_inc(pe_xz, 1)
                elif what == "z_half":
                    if later:
                        pe.wait_ge(dve_prod, k * NS)
                    for h in range(HALVES):
                        pe.matmul([H1[1], F[1]][h][:], w_in[:, DI + h * P:DI + (h + 1) * P], h_t[:, bass.ds(k * T + PRE, T)],
                                  start=True, stop=True).then_inc(pe_xz, 1)
                elif what == "xp":
                    pe.wait_ge(dve_u, k + 1)
                    for h in range(HALVES):
                        mm = pe.matmul(H3[1][:], w_xp[:, h, :], u[:, h, :], start=(h == 0), stop=(h == HALVES - 1))
                    mm.then_inc(pe_xp, 1)
                elif what == "dt":
                    pe.wait_ge(act_xp, k + 1)
                    pe.wait_ge(act_xz, 4 * k + 3)
                    for h in range(HALVES):
                        pe.matmul(H1[h][:], w_dt[:, h * P:(h + 1) * P], xps[0:RANK, :], start=True, stop=True).then_inc(pe_dt, 1)
                    pe.wait_ge(pool_stack, k + 1)
                    row_of_b(0)
                elif what == "state":
                    if i < NS - 1:
                        pe.wait_ge(act_B, k * NS + i + 1)
                        row_of_b(i + 1)
                    if i >= 2:
                        pe.wait_ge(dve_prod, k * NS + i - 1)
                    elif i == 1:
                        pe.wait_ge(act_xz, 4 * k + 4)
                    elif later:
                        pe.wait_ge(dve_lg, k)
                    pe.matmul(F[i % 2][:], pick[:, NS + i, :], stack[:], start=True, stop=True).then_inc(pe_C, 1)
                elif what == "w_out":
                    pe.wait_ge(dve_prod, k * NS + NS)
                    pe.wait_ge(dve_yg, k + 1)
                    for j in range(J):
                        for h in range(HALVES):
                            mm = pe.matmul(F[0][:, j * P:(j + 1) * P], yg[:, h, j * P:(j + 1) * P], w_out[:, h, :],
                                           start=(h == 0), stop=(h == HALVES - 1))
                    mm.then_inc(pe_wo, 1)
                elif what == "x_turn":
                    pe.wait_ge(dve_xn2, k + 1)
                    for j in range(J):
                        mm = pe.transpose(H3[0][:, j * P:(j + 1) * P], xn2[:, j, :], ident[:])
                    mm.then_inc(pe_xt, 1)
                elif what == "route":
                    pe.wait_ge(act_now, k + 1)
                    for j in range(J):
                        mm = pe.matmul(F[0][:, j * E:(j + 1) * E], x_now[:, j * P:(j + 1) * P], router[:], start=True, stop=True)
                    mm.then_inc(pe_rt, 1)
                elif what == "gate_x":
                    pe.wait_ge(pool_gated, k * E + i + 1)
                    if i == 0:
                        pe.wait_ge(act_xt, k + 1)
                    if i >= 2:
                        pe.wait_ge(act_gx, k * E + i - 1)
                    for j in range(J):
                        mm = pe.transpose(H3[i % 2][:, j * P:(j + 1) * P], gated[:, i % 2, j, :], ident[:])
                    mm.then_inc(pe_gt, 1)
                elif what == "ffn_open":
                    pe.wait_ge(dve_x2, k + 1)
                    for j in range(J):
                        mm = pe.matmul(OUT[:, j * P:(j + 1) * P], x2[:, j, :], ident[:], start=(j == 0), stop=False,
                                       skip_group_check=True)
                    mm.then_inc(pe_x2, 1)
                    pe.wait_ge(act_xt, k + 1)
                    pe.wait_ge(act_gx, k * E + E)
                elif what == "step":
                    e, m = divmod(i, len(HT))
                    M = HT[m]
                    col = e * HID + m * P
                    if i >= 2:
                        pe.wait_ge(dve_a1, k * STEPS + i - 1)
                    pe.matmul(H1[i % 2][0:M, :], w1[:, col:col + M], x_t(k), start=True, stop=True).then_inc(pe_h1, 1)
                    if i >= 2:
                        pe.wait_ge(dve_hid, k * STEPS + i - 1)
                    pe.matmul(H3[i % 2][0:M, :], w3[:, col:col + M], gx[:, e, :], start=True, stop=True).then_inc(pe_h3, 1)
                    if i >= 2:
                        down(i - 2, k)
                elif what == "ffn_close":
                    down(STEPS - 2, k)
                    down(STEPS - 1, k)
                    pe.wait_ge(act_out, k + 1)

            def row_of_b(i):
                pe.matmul(F[2][:], pick[:, i, :], stack[:], start=True, stop=True).then_inc(pe_B, 1)

            def down(i, c):
                e, m = divmod(i, len(HT))
                pe.wait_ge(dve_hid, c * STEPS + i + 1)
                pe.matmul(OUT[:], w2[0:HT[m], m, e, :], hid[0:HT[m], i % 3, :], start=False, stop=(i == STEPS - 1),
                          skip_group_check=True).then_inc(pe_w2, 1)

            pe.wait_ge(dve_xn1, 1)
            graph(0)
            pe.wait_ge(ld_cst, 16 * len(small_loads))
            graph_w(0)
            graph_turn(0)
            pe.wait_ge(ld_w, 16 * len(w_loads))
            pe.wait_ge(dve_prep, 1)
            early = {("z_half", 0): [(graph, 1, (0, 1))], ("xp", 0): [(graph, 1, (2, 3))],
                     ("state", 0): [(graph_w, 1)], ("state", 1): [(graph, 2, (0, 1))], ("state", 2): [(graph, 2, (2, 3))],
                     ("state", 3): [(graph_turn, 1)], ("state", 4): [(graph_w, 2)], ("state", 5): [(graph, 3, (0, 1))],
                     ("state", 6): [(graph, 3, (2, 3))], ("state", 7): [(graph_turn, 2)], ("state", 8): [(graph_w, 3)],
                     ("state", 10): [(graph_turn, 3)]}
            for what, i, k in seam(None, 0) + states(0):
                piece(what, i, k)
                for f, *args in early.get((what, i), []):
                    f(*args)
            for what, i, k in seam(0, 1):
                piece(what, i, k)
            pe.wait_ge(ld_ffn, 16 * len(ffn_loads))
            pe.wait_ge(dve_ffn_w, 1)
            with pe.Fori(0, CHUNKS - 2) as c:
                for what, i, k in states(c + 1, c, c) + seam(c + 1, c + 2):
                    piece(what, i, k)
            for what, i, k in states(CHUNKS - 1, CHUNKS - 2, CHUNKS - 2) + seam(CHUNKS - 1, None) + ffn_alone(CHUNKS - 1):
                piece(what, i, k)

        @block.scalar
        def _(act):
            def graph_copy(k):
                act.wait_ge(pe_adj, PIECES * (k + 1))
                if k >= 1:
                    act.wait_ge(pe_g, k)
                act.copy(z_sb[:], OUT[:]).then_inc(act_z, 1)

            def graph_ht(k):
                act.wait_ge(pe_ht, k + 1)
                act.activation(h_t[:, PRE + k * T:PRE + (k + 1) * T], H3[1][:], ACT.Identity, scale=ln_g[:], bias=ln_b[:])\
                   .then_inc(act_ht, 1)

            def piece(what, i, k):
                later = not (isinstance(k, int) and k == 0)
                if what == "x_half":
                    for h in range(HALVES):
                        act.wait_ge(pe_xz, 4 * k + h + 1)
                        act.activation(xh[:, h, :], [F[2], H1[0]][h][:], ACT.Identity, bias=conv_bh[:, h:h + 1]).then_inc(act_xz, 1)
                    act.wait_ge(act_xz, 4 * k + 2)
                    act.activation(xth[:], xh[:], ACT.Tanh).then_inc(act_xth, 1)
                elif what == "z_half":
                    for h in range(HALVES):
                        act.wait_ge(pe_xz, 4 * k + 3 + h)
                        act.copy(zh[:, h, :], [H1[1], F[1]][h][:]).then_inc(act_xz, 1)
                    act.wait_ge(act_xz, 4 * k + 4)
                    act.activation(zth[:], zh[:], ACT.Tanh).then_inc(act_zth, 1)
                elif what == "xp":
                    act.wait_ge(pe_xp, k + 1)
                    act.copy(xps[:], H3[1][:]).then_inc(act_xp, 1)
                elif what == "dt":
                    act.wait_ge(pool_sz, k + 1)
                    for h in range(HALVES):
                        act.wait_ge(pe_dt, 2 * k + h + 1)
                        act.activation(pre[:, h, :], H1[h][:], ACT.Identity, bias=b_dt[:, h:h + 1]).then_inc(act_pre, 1)
                    act.wait_ge(act_pre, 2 * k + 2)
                    act.wait_ge(dve_u, k + 1)
                    act.activation(ab[:], pre[:], ACT.Abs).then_inc(act_c, 1)
                    act.wait_ge(act_c, k + 1)
                    act.activation(ew[:], ab[:], ACT.Exp, scale=-1.0).then_inc(act_ew, 1)
                    act.wait_ge(act_ew, k + 1)
                    act.activation(ln1p[:], ew[:], ACT.Ln, bias=1.0).then_inc(act_ln, 1)
                    act.wait_ge(pe_B, k * NS + 1)
                    act.copy(b_row[:, 0, :], F[2][:]).then_inc(act_B, 1)
                elif what == "state":
                    if i == 0:
                        act.wait_ge(dve_dt, k + 1)
                    if later or i >= 3:
                        act.wait_ge(dve_scan, 2 * (k * NS + max(i - 2, 0)))
                    for h in range(HALVES):
                        act.activation(decay[:, slot3(i), h, :], dt_[:, h, :], ACT.Exp, scale=a_neg[:, h, i:i + 1]).then_inc(act_decay, 1)
                    if i < NS - 1:
                        act.wait_ge(pe_B, k * NS + i + 2)
                        if later or i >= 1:
                            act.wait_ge(pool_drive, k * NS + i)
                        act.copy(b_row[:, (i + 1) % 2, :], F[2][:]).then_inc(act_B, 1)
                    if i >= 1:
                        keep(i - 1, k)
                elif what == "gate_y":
                    keep(NS - 1, k)
                elif what == "x_turn":
                    act.wait_ge(pe_xt, k + 1)
                    if later:
                        act.wait_ge(pe_rt, k)
                    else:
                        act.wait_ge(pe_g, CHUNKS)
                    act.copy(x_now[:], H3[0][:]).then_inc(act_now, 1)
                    act.copy(x_t(k), H3[0][:]).then_inc(act_xt, 1)
                elif what == "route":
                    act.wait_ge(dve_td, k + 1)
                    act.activation(top_e[:], top_d[:], ACT.Exp).then_inc(act_te, 1)
                elif what == "gate_x":
                    act.wait_ge(pe_gt, k * E + i + 1)
                    if not later:
                        act.wait_ge(pe_adj, CHUNKS * PIECES)
                    act.copy(gx[:, i, :], H3[i % 2][:]).then_inc(act_gx, 1)
                elif what == "step":
                    M = HT[i % len(HT)]
                    act.wait_ge(pe_h1, k * STEPS + i + 1)
                    if i >= 4:
                        act.wait_ge(dve_hid, k * STEPS + i - 3)
                    act.activation(th[0:M, i % 4, :], H1[i % 2][0:M, :], ACT.Tanh).then_inc(act_th, 1)
                elif what == "ffn_close":
                    act.wait_ge(pe_w2, (k + 1) * STEPS)
                    act.copy(out_sb, OUT[:]).then_inc(act_out, 1)

            def keep(i, k):
                act.wait_ge(dve_scan, 2 * (k * NS + i + 1))
                act.copy(state[:, i, :], hs[:, slot3(i), :, T - 1]).then_inc(act_keep, 1)

            act.wait_ge(ld_cst, 16 * len(small_loads))
            act.activation(a_exp[:], a_log[:], ACT.Exp).then_inc(act_a, 1)
            graph_copy(0)
            graph_ht(0)
            early = {("xp", 0): [(graph_copy, 1)], ("state", 3): [(graph_ht, 1), (graph_copy, 2)],
                     ("state", 7): [(graph_ht, 2), (graph_copy, 3)], ("state", 10): [(graph_ht, 3)]}
            act.wait_ge(dve_prep, 1)
            for what, i, k in seam(None, 0) + states(0):
                piece(what, i, k)
                for f, n in early.get((what, i), []):
                    f(n)
            for what, i, k in seam(0, 1):
                piece(what, i, k)
            with act.Fori(0, CHUNKS - 2) as c:
                for what, i, k in states(c + 1, c, c) + seam(c + 1, c + 2):
                    piece(what, i, k)
                act.wait_ge(out_dma, 16 * (c + 1))
            for what, i, k in states(CHUNKS - 1, CHUNKS - 2, CHUNKS - 2) + seam(CHUNKS - 1, None):
                piece(what, i, k)
            act.wait_ge(out_dma, 16 * (CHUNKS - 1))
            for what, i, k in ffn_alone(CHUNKS - 1):
                piece(what, i, k)

        @block.vector
        def _(dve):
            def norm_stats(rows, stats, mv, tiles, base, done):
                for j in range(tiles):
                    dve.bn_stats(stats[:, j, :], rows[:, j, :]).then_inc(dve_c, 1)
                for j in range(tiles):
                    dve.wait_ge(dve_c, base + j + 1)
                    dve.bn_aggr(mv[:, j, :], stats[:, j, :]).then_inc(done, 1)

            def norm_rows(dst, rows, mv, rs, tiles, done):
                for j in range(tiles):
                    last = dve.tensor_scalar(dst[:, j, :], rows[:, j, :], mv[:, j, 0:1], rs[:, j:j + 1], ALU.subtract, ALU.mult)
                last.then_inc(done, 1)

            ONCE = 3 + JT
            PER_A = 1 + J
            A_ALL = ONCE + CHUNKS * PER_A

            def graph_rows(k):
                dve.wait_ge(pe_g, k + 1)
                if k >= 1:
                    dve.wait_ge(pe_ht, k)
                dve.tensor_tensor(g_pre[:], H3[0][:].rearrange("p (j c) -> p j c", j=J),
                                  over(gcn_b[:].unsqueeze(1), [P, J, D]), ALU.add).then_inc(dve_g, 1)
                dve.wait_ge(dve_g, k + 1)
                at = ONCE + k * PER_A
                dve.tensor_scalar(g_act[:], g_pre[:], 0.0, None, ALU.max).then_inc(dve_c, 1)
                dve.wait_ge(dve_c, at + 1)
                norm_stats(g_act, statsg, mvg, J, at + 1, dve_mv1)

            def graph_norm(k):
                dve.wait_ge(pool_rg, k + 1)
                norm_rows(h_nrm, g_act, mvg, rsg, J, dve_hn)

            def piece(what, i, k):
                later = not (isinstance(k, int) and k == 0)
                if what == "x_half":
                    dve.wait_ge(act_xth, k + 1)
                    dve.scalar_tensor_tensor(u[:], xth[:], 1.0, xh[:], ALU.add, ALU.mult).then_inc(dve_u, 1)
                elif what == "dt":
                    dve.wait_ge(act_ew, k + 1)
                    at = 3 * k
                    dve.tensor_scalar(low[:], ew[:], 1.0, -1.0, ALU.add, ALU.add).then_inc(own_s, 1)
                    dve.wait_ge(own_s, at + 1)
                    dve.tensor_tensor(low[:], low[:], ew[:], ALU.subtract).then_inc(own_s, 1)
                    dve.wait_ge(own_s, at + 2)
                    dve.wait_ge(act_ln, k + 1)
                    dve.wait_ge(pool_stack, k + 1)
                    dve.tensor_tensor(low[:], ln1p[:], low[:], ALU.subtract).then_inc(own_s, 1)
                    dve.wait_ge(own_s, at + 3)
                    dve.scalar_tensor_tensor(dt_[:], pre[:], 0.0, low[:], ALU.max, ALU.add).then_inc(dve_dt, 1)
                    dve.wait_ge(dve_dt, k + 1)
                    dve.tensor_tensor(dtu[:], dt_[:], u[:], ALU.mult).then_inc(dve_dtu, 1)
                elif what == "state":
                    if i >= 1:
                        weigh(i - 1, k)
                    dve.wait_ge(pool_drive, k * NS + i + 1)
                    for h in range(HALVES):
                        dve.wait_ge(act_decay, 2 * (k * NS + i) + h + 1)
                        start = state[:, i, h:h + 1] if later else 0.0
                        if h == 0 and (later or i >= 3):
                            dve.wait_ge(act_keep, k * NS + max(i - 2, 0))
                            dve.wait_ge(dve_prod, k * NS + max(i - 2, 0))
                        dve.tensor_tensor_scan(hs[:, slot3(i), h, :], decay[:, slot3(i), h, :], drive[:, i % 2, h, :], start,
                                               ALU.mult, ALU.add).then_inc(dve_scan, 1)
                elif what == "gate_y":
                    weigh(NS - 1, k)
                    own_add(NS - 1, k)
                    dve.wait_ge(own_y, own_before(k) + len(own_states(k)) - 1)
                    for h in range(HALVES):
                        dve.scalar_tensor_tensor(yown[:, h, :], u[:, h, :], d_skip[:, h:h + 1], yown[:, h, :], ALU.mult, ALU.add)\
                           .then_inc(own_d, 1)
                    dve.wait_ge(own_d, 2 * k + 2)
                    dve.wait_ge(pool_y, adds_before(k + 1))
                    dve.tensor_tensor(yacc[:], yacc[:], yown[:], ALU.add).then_inc(own_sum, 1)
                    dve.wait_ge(own_sum, k + 1)
                    dve.wait_ge(pool_sz, k + 1)
                    dve.tensor_tensor(yg[:], yacc[:], sz[:], ALU.mult).then_inc(dve_yg, 1)
                elif what == "w_out":
                    dve.wait_ge(pe_wo, k + 1)
                    if later:
                        dve.wait_ge(pe_x2, k)
                    dve.tensor_tensor(x2, F[0][:].rearrange("p (j c) -> p j c", j=J),
                                      x_sb[:, bass.ds(k * J, J), :], ALU.add).then_inc(dve_x2, 1)
                    dve.wait_ge(dve_x2, k + 1)
                    for j in range(J):
                        last = dve.bn_stats(stats2[:, j, :], x2[:, j, :])
                    last.then_inc(own_n, 1)
                    for j in range(J):
                        dve.wait_ge(ld_x, 16)
                        dve.wait_ge(own_n, k + 1)
                        dve.bn_aggr(mv2[:, j, :], stats2[:, j, :]).then_inc(dve_mv2, 1)
                elif what == "x_turn":
                    dve.wait_ge(pool_r2, k + 1)
                    norm_rows(xn2, x2, mv2, rs2, J, dve_xn2)
                elif what == "route":
                    route(k)
                elif what == "step":
                    M = HT[i % len(HT)]
                    dve.wait_ge(act_th, k * STEPS + i + 1)
                    dve.scalar_tensor_tensor(th[0:M, i % 4, :], th[0:M, i % 4, :], 1.0, H1[i % 2][0:M, :], ALU.add, ALU.mult)\
                       .then_inc(dve_a1, 1)
                    if i >= 1:
                        hidden(i - 1, k)
                elif what == "ffn_close":
                    hidden(STEPS - 1, k)

            def hidden(i, k):
                M = HT[i % len(HT)]
                dve.wait_ge(dve_a1, k * STEPS + i + 1)
                dve.wait_ge(pe_h3, k * STEPS + i + 1)
                if i >= 3:
                    dve.wait_ge(pe_w2, k * STEPS + i - 2)
                dve.tensor_tensor(hid[0:M, i % 3, :], th[0:M, i % 4, :], H3[i % 2][0:M, :], ALU.mult).then_inc(dve_hid, 1)

            def own_before(k):
                return 0 if isinstance(k, int) and k == 0 else len(OWN_ALONE) - 1 + (k - 1) * (len(OWN_BESIDE) - 1)

            def weigh(i, k):
                later = not (isinstance(k, int) and k == 0)
                own = own_states(k)
                c_row = over(F[i % 2][:].unsqueeze(1), [P, HALVES, T])
                if i - 1 in own:
                    own_add(i - 1, k)
                dve.wait_ge(pe_C, k * NS + i + 1)
                dve.wait_ge(dve_scan, 2 * (k * NS + i + 1))
                if i in own:
                    if own.index(i) >= 2:
                        dve.wait_ge(own_y, own_before(k) + own.index(i) - 1)
                    ins = dve.tensor_tensor(yown[:] if i == own[0] else ptmp[:], hs[:, slot3(i)], c_row, ALU.mult)
                else:
                    nth = [n for n in range(NS) if n not in own].index(i)
                    if nth == 0:
                        if later:
                            dve.wait_ge(pe_wo, k)
                        dst = yacc[:]
                    else:
                        dst = prod[:, nth % 2]
                        if later or nth >= 3:
                            dve.wait_ge(pool_y, adds_before(k) + max(nth - 2, 0))
                    ins = dve.tensor_tensor(dst, hs[:, slot3(i)], c_row, ALU.mult)
                ins.then_inc(dve_prod, 1)

            def own_add(i, k):
                own = own_states(k)
                nth = own.index(i)
                dve.wait_ge(dve_prod, k * NS + i + 1)
                if nth == 0:
                    return
                if nth >= 2:
                    dve.wait_ge(own_y, own_before(k) + nth - 1)
                dve.tensor_tensor(yown[:], yown[:], ptmp[:], ALU.add).then_inc(own_y, 1)

            def route(k):
                n = [0]

                def own(ins):
                    n[0] += 1
                    ins.then_inc(own_r, 1)
                    dve.wait_ge(own_r, ROUTE * k + n[0])

                dve.wait_ge(pe_rt, k + 1)
                dve.tensor_copy(logits[:], F[0][:, 0:J * E].rearrange("p (j e) -> p j e", j=J)).then_inc(dve_lg, 1)
                for j in range(J):
                    dve.wait_ge(ld_x, 16)
                    dve.wait_ge(dve_lg, k + 1)
                    dve.max(top[:, j, :], logits[:, j, :]).then_inc(own_r, 1)
                dve.wait_ge(own_r, ROUTE * k + J)
                dve.tensor_tensor(top_d[:], top[:], over(top[:, :, 0:1], [P, J, 8]), ALU.subtract).then_inc(dve_td, 1)
                for j in range(J):
                    dve.max_index(top_at[:, j, :], top[:, j, :], logits[:, j, :]).then_inc(own_r, 1)
                n[0] = 2 * J
                dve.wait_ge(own_r, ROUTE * k + 2 * J)
                own(dve.tensor_copy(at_f[:], top_at[:, :, 0:2]))
                own(dve.tensor_tensor(eq0, over(iota[:].unsqueeze(1), [P, J, E]), over(at_f[:, :, 0:1], [P, J, E]), ALU.is_equal))
                own(dve.tensor_tensor(eq1, over(iota[:].unsqueeze(1), [P, J, E]), over(at_f[:, :, 1:2], [P, J, E]), ALU.is_equal))
                dve.wait_ge(act_te, k + 1)
                own(dve.tensor_reduce(zsum[:], top_e[:], mybir.AxisListType.X, ALU.add))
                own(dve.reciprocal(rz[:], zsum[:]))
                own(dve.tensor_tensor(prob[:], top_e[:, :, 0:2], over(rz[:], [P, J, 2]), ALU.mult))
                own(dve.tensor_tensor(psum2[:], prob[:, :, 0:1], prob[:, :, 1:2], ALU.add))
                own(dve.tensor_scalar(psum2[:], psum2[:], 1e-9, None, ALU.add))
                own(dve.reciprocal(rp[:], psum2[:]))
                own(dve.tensor_tensor(gate2[:], prob[:], over(rp[:], [P, J, 2]), ALU.mult))
                own(dve.tensor_tensor(eq0, eq0, over(gate2[:, :, 0:1], [P, J, E]), ALU.mult))
                own(dve.tensor_tensor(eq1, eq1, over(gate2[:, :, 1:2], [P, J, E]), ALU.mult))
                dve.tensor_tensor(gate, eq0, eq1, ALU.add).then_inc(dve_gate, 1)
                assert n[0] == ROUTE

            own_s, own_y, own_n, own_r, own_d, own_sum = [sem(n) for n in ("own_s", "own_y", "own_n", "own_r", "own_d", "own_sum")]
            ROUTE = 20

            dve.wait_ge(ld_x, 16)
            norm_stats(x_sb, stats1, mv1, JT, 0, dve_mv1)
            dve.wait_ge(pool_r1, 1)
            norm_rows(xn1, x_sb, mv1, rs1, JT, dve_xn1)
            dve.wait_ge(ld_cst, 16 * len(small_loads))
            dve.wait_ge(act_a, 1)
            dve.tensor_scalar(a_neg[:], a_exp[:], -1.0, None, ALU.mult).then_inc(dve_c, 1)
            dve.tensor_scalar(conv_bh[:], conv_b[:], 0.5, None, ALU.mult).then_inc(dve_c, 1)
            dve.wait_ge(ld_w, 16 * len(w_loads))
            dve.scalar_tensor_tensor(w_tap[:], conv_wb[:], 0.5, over(w_in[:, 0:DI].unsqueeze(1), [P, TAPS, DI]), ALU.mult, ALU.mult)\
               .then_inc(dve_c, 1)
            dve.tensor_scalar(w_in[:, DI:2 * DI], w_in[:, DI:2 * DI], 0.5, None, ALU.mult).then_inc(dve_halved, 1)
            dve.wait_ge(dve_c, ONCE)
            dve.wait_ge(dve_halved, 1)
            dve.wait_ge(pool_set, 7)
            dve.engine_nop().then_inc(dve_prep, 1)
            graph_rows(0)
            graph_norm(0)
            early = {("state", 1): [(graph_rows, 1)], ("state", 2): [(graph_norm, 1)],
                     ("state", 5): [(graph_rows, 2)], ("state", 6): [(graph_norm, 2)],
                     ("state", 8): [(graph_rows, 3)], ("state", 9): [(graph_norm, 3)]}
            for what, i, k in seam(None, 0) + states(0):
                piece(what, i, k)
                for f, n in early.get((what, i), []):
                    f(n)
            for what, i, k in seam(0, 1):
                piece(what, i, k)
            dve.wait_ge(ld_ffn, 16 * len(ffn_loads))
            dve.tensor_scalar(w1[:], w1[:], 0.5, None, ALU.mult).then_inc(dve_ffn_w, 1)
            with dve.Fori(0, CHUNKS - 2) as c:
                for what, i, k in states(c + 1, c, c) + seam(c + 1, c + 2):
                    piece(what, i, k)
            for what, i, k in states(CHUNKS - 1, CHUNKS - 2, CHUNKS - 2) + seam(CHUNKS - 1, None) + ffn_alone(CHUNKS - 1):
                piece(what, i, k)

        @block.gpsimd
        def _(pool):
            def rstd(mv, ve, rs, own_at, done):
                pool.tensor_scalar(ve[:], mv[:, :, 1], EPS, None, ALU.add).then_inc(pool_c, 1)
                pool.wait_ge(pool_c, own_at + 1)
                n = ve.shape[1]
                pool.tensor_tensor(rs[:], ve[:], minus_half[:, 0:n], ALU.pow).then_inc(done, 1)

            def graph_r(k):
                pool.wait_ge(dve_mv1, JT + (k + 1) * J)
                rstd(mvg, veg, rsg, 1 + k, pool_rg)

            def piece(what, i, k):
                later = not (isinstance(k, int) and k == 0)
                if what == "z_half":
                    pool.wait_ge(act_zth, k + 1)
                    if later:
                        pool.wait_ge(dve_yg, k)
                    pool.tensor_tensor(zth[:], zth[:], over(one[:].unsqueeze(2), [P, HALVES, T]), ALU.add).then_inc(own_z, 1)
                    pool.wait_ge(own_z, k + 1)
                    pool.tensor_tensor(sz[:], zth[:], zh[:], ALU.mult).then_inc(pool_sz, 1)
                elif what == "xp":
                    pool.wait_ge(act_xp, k + 1)
                    if later:
                        pool.wait_ge(pe_C, k * NS)
                    at = 4 * k
                    pool.tensor_tensor(stack[:], xps[:], over(one[:, 0:1], [P, T]), ALU.mult).then_inc(own_b, 1)
                    pool.wait_ge(own_b, at + 1)
                    pool.tensor_tensor(rest[64:128, :], xps[64:128, :], stack[64:128, :], ALU.subtract).then_inc(own_b, 1)
                    pool.wait_ge(own_b, at + 2)
                    pool.tensor_tensor(stack[64:128, :], rest[64:128, :], over(one[64:128, 0:1], [64, T]), ALU.mult).then_inc(own_b, 1)
                    pool.wait_ge(own_b, at + 3)
                    pool.tensor_tensor(rest[96:128, :], rest[96:128, :], stack[96:128, :], ALU.subtract).then_inc(own_b, 1)
                    pool.wait_ge(own_b, at + 4)
                    pool.tensor_tensor(stack[96:128, :], rest[96:128, :], over(one[96:128, 0:1], [32, T]), ALU.mult).then_inc(pool_stack, 1)
                elif what == "dt":
                    pool.wait_ge(pool_stack, k + 1)
                elif what == "state":
                    if i == 0:
                        pool.wait_ge(dve_dtu, k + 1)
                    pool.wait_ge(act_B, k * NS + i + 1)
                    if later or i >= 2:
                        pool.wait_ge(dve_scan, 2 * (k * NS + max(i - 1, 0)))
                    pool.tensor_tensor(drive[:, i % 2], dtu[:], over(b_row[:, i % 2, :].unsqueeze(1), [P, HALVES, T]), ALU.mult)\
                        .then_inc(pool_drive, 1)
                    if i >= 2:
                        add(i - 2, k)
                elif what == "gate_y":
                    add(NS - 2, k)
                    add(NS - 1, k)
                elif what == "w_out":
                    pool.wait_ge(dve_mv2, (k + 1) * J)
                    pool.tensor_tensor(ve2[:], mv2[:, :, 1], eps_row[:], ALU.add).then_inc(pool_c2, 1)
                    pool.wait_ge(pool_c2, k + 1)
                    pool.tensor_tensor(rs2[:], ve2[:], minus_half[:, 0:J], ALU.pow).then_inc(pool_r2, 1)
                elif what == "gate_x":
                    if i == 0:
                        pool.wait_ge(dve_gate, k + 1)
                    if later or i >= 2:
                        pool.wait_ge(pe_gt, k * E + max(i - 1, 0))
                    pool.tensor_tensor(gated[:, i % 2], xn2, over(gate[:, :, i:i + 1], [P, J, D]), ALU.mult)\
                        .then_inc(pool_gated, 1)

            def add(i, k):
                ours = [n for n in range(NS) if n not in own_states(k)]
                if i not in ours[1:]:
                    return
                nth = ours.index(i)
                pool.wait_ge(dve_prod, k * NS + i + 1)
                if nth >= 2:
                    pool.wait_ge(pool_y, adds_before(k) + nth - 1)
                pool.tensor_tensor(yacc[:], yacc[:], prod[:, nth % 2], ALU.add).then_inc(pool_y, 1)

            own_z, own_b = sem("own_z"), sem("own_b")
            pool.memset(minus_half[:], -0.5).then_inc(pool_set, 1)
            pool.memset(w_xp[:, :, RANK:BC0], 0.0).then_inc(pool_set, 1)
            pool.memset(h_t[:, 0:PRE], 0.0).then_inc(pool_set, 1)
            pool.memset(eps_row[:], EPS).then_inc(pool_set, 1)
            pool.memset(one[:], 1.0).then_inc(pool_set, 1)
            pool.wait_ge(pool_set, 5)
            pool.wait_ge(dve_mv1, JT)
            rstd(mv1, ve1, rs1, 0, pool_r1)
            pool.wait_ge(ld_cst, 16 * len(small_loads))
            pool.tensor_copy(pick[:, 0:NS], over(pick_f[:, 0:NS].unsqueeze(2), [P, NS, P])).then_inc(pool_set, 1)
            pool.tensor_copy(pick[:, NS:2 * NS], over(pick_f[:, NS:2 * NS].unsqueeze(2), [P, NS, P])).then_inc(pool_set, 1)
            graph_r(0)
            early = {("state", 1): [(graph_r, 1)], ("state", 5): [(graph_r, 2)], ("state", 8): [(graph_r, 3)]}
            for what, i, k in seam(None, 0) + states(0):
                piece(what, i, k)
                for f, n in early.get((what, i), []):
                    f(n)
            for what, i, k in seam(0, 1):
                piece(what, i, k)
            with pool.Fori(0, CHUNKS - 2) as c:
                for what, i, k in states(c + 1, c, c) + seam(c + 1, c + 2):
                    piece(what, i, k)
            for what, i, k in states(CHUNKS - 1, CHUNKS - 2, CHUNKS - 2) + seam(CHUNKS - 1, None) + ffn_alone(CHUNKS - 1):
                piece(what, i, k)


def slot3(i):
    return i % 3


def kernel(x, adj, L0_gnn_gcn_w, L0_gnn_gcn_b, L0_gnn_ln_g, L0_gnn_ln_b, L0_gnn_w_in, L0_gnn_conv_w,
           L0_gnn_conv_b, L0_gnn_w_xp, L0_gnn_w_dt, L0_gnn_b_dt, L0_gnn_A_log, L0_gnn_D_skip, L0_gnn_w_out,
           L0_ffn_router_w, L0_ffn_w1, L0_ffn_w2, L0_ffn_w3):
    import numpy as np
    import concourse.bacc as bacc
    from concourse.bass_utils import run_bass_kernel_spmd

    def tiles(a):
        a = np.asarray(a)
        return a.reshape(-1, P, a.shape[1]).transpose(1, 0, 2)

    def channels(v):
        return np.asarray(v).reshape(HALVES, P).T

    pick = np.zeros((P, 2 * NS), np.float32)
    for r in range(3):
        pick[BC0 + 32 * r:BC0 + 32 * r + 32, :] = np.eye(2 * NS, dtype=np.float32)
    arrays = {
        "x": tiles(x),
        "adj": np.asarray(adj).reshape(CHUNKS, T, JT, P).transpose(0, 3, 2, 1),
        "gcn_w": L0_gnn_gcn_w, "gcn_b": L0_gnn_gcn_b,
        "ln_g": np.asarray(L0_gnn_ln_g).reshape(D, 1), "ln_b": np.asarray(L0_gnn_ln_b).reshape(D, 1),
        "w_in": L0_gnn_w_in, "conv_w": np.asarray(L0_gnn_conv_w).T, "conv_b": channels(L0_gnn_conv_b),
        "w_xp": L0_gnn_w_xp, "w_dt": L0_gnn_w_dt, "b_dt": channels(L0_gnn_b_dt),
        "A_log": L0_gnn_A_log, "D_skip": channels(L0_gnn_D_skip), "w_out": L0_gnn_w_out,
        "router": np.asarray(L0_ffn_router_w).T,
        "w1": np.asarray(L0_ffn_w1).reshape(E * HID, D).T,
        "w3": np.asarray(L0_ffn_w3).reshape(E * HID, D).T,
        "w2": np.asarray(L0_ffn_w2).transpose(2, 0, 1),
        "identity": np.eye(P, dtype=np.float32),
        "pick": pick,
        "iota": np.arange(E, dtype=np.float32),
    }
    nc = bacc.Bacc("TRN2", target_bir_lowering=False, num_devices=1)
    sent, args = {}, {}
    for name, a in arrays.items():
        a = np.ascontiguousarray(a)
        sent[f"in_{name}"] = a
        args[name] = nc.dram_tensor(f"in_{name}", a.shape, mybir.dt.from_np(a.dtype), kind="ExternalInput").ap()
    out = nc.dram_tensor("out_t", (D, L), F32, kind="ExternalOutput").ap()
    build_kernel(nc, args, out)
    result = run_bass_kernel_spmd(nc, [sent], core_ids=[0])
    return np.ascontiguousarray(result.results[0]["out_t"].T)
```

```python
from contextlib import ExitStack

import concourse.bass as bass
from concourse import mybir

F32 = mybir.dt.float32
BF16 = mybir.dt.bfloat16
U32 = mybir.dt.uint32
ALU = mybir.AluOpType
ACT = mybir.ActivationFunctionType

P = 128
L = 2048
D = 128
DI = 256
HALVES = DI // P
NS = 16
RANK = 8
TAPS = 4
E = 8
HID = 341
EPS = 1e-5

T = 512
CHUNKS = L // T
J = T // P
JT = L // P
PIECE = 4
PIECES = JT // PIECE
HT = [128, 128, HID - 256]
STEPS = E * len(HT)
BC0 = 32
PRE = TAPS - 1


OWN_ALONE = (2, 3, 5, 6, 8, 10, 14, 15)
OWN_BESIDE = (3, 5, 8, 10, 14, 15)


def first(k):
    return isinstance(k, int) and k == 0


def own_states(k):
    return OWN_ALONE if first(k) else OWN_BESIDE


def shared(n_own):
    return NS - n_own - 1


def adds_before(k):
    return 0 if first(k) else shared(len(OWN_ALONE)) + (k - 1) * shared(len(OWN_BESIDE))


def own_before(k):
    return 0 if first(k) else len(OWN_ALONE) + 1 + (k - 1) * (len(OWN_BESIDE) + 1)


SPARE_USERS = ("graph_g", "graph_turn", "x", "z", "xp", "dt", "w_out", "x_turn", "route", "gate_x")
AFTER = {"u": ("x", 1), "graph_rows": ("graph_g", 0), "norm": ("w_out", 0)}
ORDER = {
    "first": {
        "pe": """
            graph:0-3@0 graph_g:0@0 graph:0@1 graph_turn:0@0 graph:1@1 x:0-1 xp:0 dt:0-1 graph:2-3@1 z:0
            graph:0@2 row_b:0 row_c:0 graph:1@2 row_b:1 graph_g:0@1 row_b:2 z:1 row_c:1 row_b:3-4 row_c:2
            row_b:5 graph_turn:0@1 row_c:3 row_b:6 x:0> row_c:4 row_b:7 graph:2@2 row_c:5 graph:3@2 row_c:6
            row_b:8 x:1> graph:0@3 graph_g:0@2 row_c:7 row_b:9 graph:1@3 row_c:8 row_b:10 graph:2@3 row_c:9
            row_b:11 xp:0> graph:3@3 graph_turn:0@2 row_c:10 row_b:12 graph_g:0@3 row_c:11 row_b:13 dt:0>
            row_b:14 row_c:12 dt:1> graph_turn:0@3 row_c:13 row_b:15 row_c:14-15 row_b:0-3> row_c:0> row_b:4>
            w_out:0 row_c:1> x_turn:0 route:0 row_c:2-3>""",
        "act": """
            graph_z:0@0 graph_g:0@0 graph_turn:0@0 x:0-1 u:0 xp:0 dt:0-1 graph_z:0@1 decay:0 skip:0 decay:1
            row_b:0 z:0 row_b:1 graph_g:0@1 keep:0 row_b:2 decay:2 row_b:3 z:1 keep:1 decay:3 row_b:4 keep:2
            decay:4 row_b:5 graph_turn:0@1 keep:3 decay:5 row_b:6 keep:4 decay:6 x:0> row_b:7 keep:5 decay:7
            graph_z:0@2 keep:6 row_b:8 decay:8 x:1> keep:7 u:0> decay:9 graph_g:0@2 row_b:9-10 keep:8 decay:10
            keep:9 decay:11 row_b:11 xp:0> keep:10 decay:12 graph_z:0@3 graph_turn:0@2 row_b:12 graph_g:0@3
            keep:11 row_b:13 decay:13 dt:0-1> graph_turn:0@3 keep:12 row_b:14 decay:14 keep:13 row_b:15
            decay:15 keep:14 decay:0> row_b:0-2> keep:15 decay:1> row_b:3> keep:0> decay:2> row_b:4> x_turn:0
            keep:1> decay:3> route:0 keep:2> decay:4> top_exp:0""",
        "dve": """
            graph_rows:0@0 graph_norm:0@0 u:0 soft:0-1 turn_over:0 scan:0 weigh:0 graph_rows:0@1 scan:1 weigh:1
            scan:2 graph_norm:0@1 weigh:2 scan:3 weigh:3 scan:4 weigh:4 scan:5 weigh:5 scan:6 weigh:6 scan:7
            u:0> weigh:7 graph_rows:0@2 scan:8 weigh:8 scan:9 graph_norm:0@2 weigh:9 scan:10 weigh:10 scan:11
            weigh:11 graph_rows:0@3 graph_norm:0@3 scan:12 weigh:12 scan:13 soft:0> weigh:13 soft:1> scan:14
            weigh:14 turn_over:0> scan:15 weigh:15 gate_y:0 scan:0> norm:0 weigh:0> x_turn:0 scan:1> weigh:1>
            scan:2> route:0 weigh:2> scan:3>""",
        "pool": """
            graph_rows:0@0 xp:0 drive:0-2 graph_rows:0@1 drive:3 add:1 drive:4-5 z:1 drive:6-7 add:4 drive:8-9
            add:7 graph_rows:0@2 drive:10-11 add:9 xp:0> graph_rows:0@3 drive:12-13 add:11-12 drive:14-15
            add:13 drive:0-2> norm:0 drive:3> add:1> drive:4>""",
    },
    "loop": {
        "pe": """
            ffn_open:0< gate_x:0< row_b:5 z:0 step:0< gate_x:1< row_c:4 step:1< row_b:6 z:1 row_c:5 row_b:7
            x:0> step:2< gate_x:2< row_c:6 step:3< x:1> step:4< gate_x:3< row_b:8 step:5< row_c:7 row_b:9
            gate_x:4< step:6< row_c:8 row_b:10 xp:0> step:7< row_c:9 gate_x:5< step:8< row_b:11 dt:0> step:9<
            gate_x:6< row_c:10 step:10< dt:1> row_b:12 row_c:11 step:11< gate_x:7< row_c:12 row_b:13
            step:12-13< row_b:14 row_c:13 step:14< row_b:15 row_c:14 step:15< row_c:15 step:16< row_b:0>
            step:17< row_b:1-2> step:18< w_out:0 step:19< row_c:0> row_b:3> step:20< x_turn:0 row_c:1> row_b:4>
            step:21-22< row_c:2> route:0 step:23< row_c:3> ffn_close:0<""",
        "act": """
            skip:0 keep:3 decay:5 gate_x:0< row_b:5 z:0 keep:4 decay:6 step:0< gate_x:1< step:1< row_b:6 z:1
            row_b:7 keep:5 decay:7 x:0> step:2< keep:6 decay:8 gate_x:2< step:3< keep:7 decay:9 x:1> step:4<
            u:0> gate_x:3< row_b:8 step:5< row_b:9 gate_x:4< step:6< keep:8 decay:10 row_b:10 xp:0> step:7<
            keep:9 decay:11 gate_x:5< step:8< row_b:11 dt:0> step:9< gate_x:6< step:10< keep:10 decay:12 dt:1>
            step:11< row_b:12 gate_x:7< keep:11 row_b:13 decay:13 step:12< keep:12 decay:14 step:13< keep:13
            decay:15 row_b:14 step:14< row_b:15 step:15< keep:14 step:16< decay:0> row_b:0> step:17< row_b:1>
            keep:15 decay:1> row_b:2> step:18< keep:0> decay:2> step:19< row_b:3> step:20< keep:1> x_turn:0
            decay:3> row_b:4> step:21< keep:2> decay:4> step:22< route:0 step:23< top_exp:0 ffn_out:0<""",
        "dve": """
            weigh:3 scan:4 weigh:4 step:0-1< scan:5 weigh:5 scan:6 step:2< weigh:6 step:3< scan:7 step:4< u:0>
            step:5< weigh:7 scan:8 step:6< weigh:8 scan:9 step:7< weigh:9 step:8-9< scan:10 weigh:10 step:10<
            scan:11 weigh:11 soft:0> step:11< soft:1> scan:12 step:12< weigh:12 scan:13 step:13< weigh:13
            step:14< scan:14 weigh:14 step:15< turn_over:0> step:16< scan:15 step:17< weigh:15 gate_y:0
            step:18< scan:0> norm:0 step:19< weigh:0> x_turn:0 scan:1> step:20< weigh:1> scan:2> step:21-22<
            weigh:2> scan:3> step:23< ffn_close:0< route:0""",
        "pool": """
            gated:0< add:2 gated:1-2< drive:5 gated:3< add:4 drive:6-7 z:1 gated:4< add:6 gated:5< drive:8
            gated:6< drive:9 add:7 xp:0> drive:10-11 add:9 gated:7< add:11 drive:12-13 add:12 drive:14 add:13
            drive:15 drive:0-2> norm:0 drive:3> add:1> drive:4>""",
    },
    "last": {
        "pe": """
            z:0 row_b:5 ffn_open:0< row_c:4 gate_x:0< row_b:6 gate_x:1< step:0-1< z:1 row_c:5 row_b:7 gate_x:2<
            step:2< row_c:6 gate_x:3< row_b:8 step:3< row_c:7 row_b:9 step:4< row_b:10 row_c:8 step:5<
            gate_x:4< row_c:9 row_b:11 step:6< row_b:12 step:7< row_c:10 row_b:13 step:8< gate_x:5< row_c:11
            step:9< gate_x:6< row_b:14 row_c:12 row_b:15 step:10< gate_x:7< row_c:13 step:11-12< row_c:14
            step:13-14< row_c:15 step:15< w_out:0 step:16-18< x_turn:0 step:19< route:0 step:20-22< gate_x:0
            step:23< gate_x:1 ffn_close:0< gate_x:2 ffn_open:0 step:0-1 gate_x:3-4 step:2-3 gate_x:5 step:4-5
            gate_x:6 step:6-8 gate_x:7 step:9-23 ffn_close:0""",
        "act": """
            skip:0 z:0 keep:3 row_b:5 gate_x:0< decay:5 gate_x:1< step:0< keep:4 row_b:6 decay:6 step:1< z:1
            gate_x:2< keep:5 step:2< row_b:7 decay:7 gate_x:3< keep:6 row_b:8 step:3< decay:8 row_b:9 step:4<
            keep:7 decay:9 row_b:10 step:5< keep:8 decay:10 gate_x:4< row_b:11 step:6< keep:9 decay:11 step:7<
            row_b:12 step:8< keep:10 decay:12 gate_x:5< row_b:13 step:9< keep:11 decay:13 gate_x:6< row_b:14
            step:10< keep:12 decay:14 row_b:15 step:11< keep:13 decay:15 gate_x:7< step:12< keep:14 step:13-14<
            keep:15 step:15-18< x_turn:0 step:19< route:0 top_exp:0 step:20-22< gate_x:0 step:23< gate_x:1
            ffn_out:0< gate_x:2 step:0-1 gate_x:3 step:2 gate_x:4 step:3-5 gate_x:5 step:6-8 gate_x:6 step:9-11
            gate_x:7 step:12-23 ffn_out:0""",
        "dve": """
            weigh:3 scan:4 weigh:4 scan:5 step:0-1< weigh:5 scan:6 step:2< weigh:6 step:3< scan:7 weigh:7
            step:4< scan:8 weigh:8 step:5< scan:9 step:6< weigh:9 step:7< scan:10 weigh:10 step:8< scan:11
            weigh:11 step:9< scan:12 weigh:12 step:10< scan:13 step:11< weigh:13 step:12< scan:14 weigh:14
            step:13< scan:15 step:14< weigh:15 gate_y:0 step:15< norm:0 step:16< x_turn:0 step:17-19< route:0
            step:20-23< ffn_close:0< step:0-23 ffn_close:0""",
        "pool": """
            add:2 gated:0-1< drive:5 gated:2-3< drive:6 add:4 drive:7 z:1 drive:8 gated:4< drive:9 add:6
            drive:10 add:7 gated:5< drive:11 gated:6< drive:12 add:9 gated:7< drive:13-14 add:11 drive:15
            add:12-13 norm:0 gated:0-7""",
    },
}


def pieces(name, engine, former, own, following):
    out = []
    for token in ORDER[name][engine].split():
        what, rest = token.split(":")
        rest, _, fixed = rest.partition("@")
        chunk = int(fixed) if fixed else former if rest.endswith("<") else following if rest.endswith(">") else own
        low, _, high = rest.strip("<>").partition("-")
        out += [(what, i, chunk) for i in range(int(low), int(high or low) + 1)]
    return out


def numbered(order, spare_order, before):
    held = {piece: n for n, piece in enumerate(piece for piece in spare_order if piece[0] in SPARE_USERS)}
    out = []
    for what, i, chunk in order:
        if what in SPARE_USERS:
            n = held[what, i, chunk]
        elif what == "step":
            n = held["gate_x", i // len(HT), chunk] + 1
        elif what in AFTER:
            n = held[AFTER[what] + (chunk,)] + 1
        else:
            n = 0
        out.append((what, i, chunk, before + n))
    return out


def spares(order):
    return sum(piece[0] in SPARE_USERS for piece in order)


def program(engine):
    head = {e: pieces("first", e, None, 0, 1) for e in ("pe", engine)}
    body = {e: pieces("loop", e, "former", "own", "following") for e in ("pe", engine)}
    tail = {e: pieces("last", e, CHUNKS - 2, CHUNKS - 1, None) for e in ("pe", engine)}
    per_head, per_body = spares(head["pe"]), spares(body["pe"])

    def loop(c):
        chunk = {"former": c, "own": c + 1, "following": c + 2}
        return [(what, i, chunk[role], held + per_body * c) for what, i, role, held in numbered(body[engine], body["pe"], per_head)]
    return (numbered(head[engine], head["pe"], 0), loop,
            numbered(tail[engine], tail["pe"], per_head + per_body * (CHUNKS - 2)))


def build_kernel(nc, A, out):
    with ExitStack() as ctx:
        def sb(name, shape, dt=F32):
            return ctx.enter_context(nc.sbuf_tensor(name, shape, dt))

        def sem(name):
            return ctx.enter_context(nc.semaphore(name))

        def bank(name):
            return ctx.enter_context(nc.psum_tensor(name, [P, T], F32))

        xn = sb("xn", [P, JT, D])
        adj_sb = sb("adj_sb", [P, 2, PIECE, T])
        x_res = sb("x_res", [P, J, D])
        x2 = sb("x2", [P, J, D])
        xn2 = sb("xn2", [P, J, D])
        gated = sb("gated", [P, 2, J, D])
        gx = sb("gx", [P, 4, T])
        th = sb("th", [P, 4, T])
        hid = sb("hid", [P, 3, T])
        out_sb = sb("out_sb", [P, T])
        gcn_w = sb("gcn_w", [D, D])
        gcn_b = sb("gcn_b", [1, D])
        ones_row = sb("ones_row", [1, P])
        ln_g = sb("ln_g", [D, 1])
        ln_b = sb("ln_b", [D, 1])
        w_in = sb("w_in", [D, 2 * DI])
        conv_wb = sb("conv_wb", [P, TAPS, DI])
        b_row = conv_wb[:].rearrange("p (a b) d -> p a (b d)", a=2)
        w_tap = sb("w_tap", [D, TAPS, DI])
        conv_b = sb("conv_b", [P, HALVES])
        conv_bh = sb("conv_bh", [P, HALVES])
        w_xp = sb("w_xp", [P, HALVES, P])
        w_dt = sb("w_dt", [RANK, DI])
        b_dt = sb("b_dt", [P, HALVES])
        a_log = sb("a_log", [P, HALVES, NS])
        a_exp = sb("a_exp", [P, HALVES, NS])
        a_neg = sb("a_neg", [P, HALVES, NS])
        d_skip = sb("d_skip", [P, HALVES])
        w_out = sb("w_out", [P, HALVES, D])
        router = sb("router", [D, E])
        w1 = sb("w1", [D, E * HID])
        w3 = sb("w3", [D, E * HID])
        w2 = sb("w2", [P, len(HT), E, D])
        ident = sb("ident", [P, P])
        pick_f = sb("pick_f", [P, 2 * NS])
        pick = sb("pick", [P, 2 * NS], BF16)
        iota = sb("iota", [P, E])
        minus_half = sb("minus_half", [P, JT])
        eps_row = sb("eps_row", [P, JT])
        one = sb("one", [P, HALVES])

        stats1 = sb("stats1", [P, JT, 6])
        mv1 = sb("mv1", [P, JT, 2])
        ve1 = sb("ve1", [P, JT])
        rs1 = sb("rs1", [P, JT])
        z_sb = sb("z_sb", [D, T])
        g_act = sb("g_act", [P, J, D])
        statsg = sb("statsg", [P, J, 6])
        mvg = sb("mvg", [P, J, 2])
        veg = sb("veg", [P, J])
        rsg = sb("rsg", [P, J])
        h_nrm = sb("h_nrm", [P, J, D])
        h_t = sb("h_t", [D, PRE + L])

        def x_t(k):
            return h_t[:, bass.ds(k * T, T)]

        xh = sb("xh", [P, HALVES, T])
        xth = sb("xth", [P, HALVES, T])
        zh = sb("zh", [P, HALVES, T])
        zth = sb("zth", [P, HALVES, T])
        u = sb("u", [P, HALVES, T])
        sz = sb("sz", [P, HALVES, T])
        xps = sb("xps", [P, T])
        stack = sb("stack", [P, T], BF16)
        pre, ab, ew, ln1p, low = zh, xth, zth, xth, xh
        rest = xh[:, 0, :]
        stack_next = sb("stack_next", [P, T], BF16)
        dt_ = sb("dt_", [P, HALVES, T])
        dtu = sb("dtu", [P, HALVES, T])
        decay = sb("decay", [P, 2, HALVES, T])
        drive = sb("drive", [P, 2, HALVES, T])
        hs = sb("hs", [P, 2, HALVES, T])
        state = sb("state", [P, NS, HALVES])
        prod = sb("prod", [P, 2, HALVES, T])
        yacc = sb("yacc", [P, HALVES, T])
        yg = yacc
        yown = sb("yown", [P, HALVES, T])
        ptmp = sb("ptmp", [P, HALVES, T])
        stats2 = sb("stats2", [P, J, 6])
        mv2 = sb("mv2", [P, J, 2])
        ve2 = sb("ve2", [P, J])
        rs2 = sb("rs2", [P, J])
        x_now = sb("x_now", [D, T])
        logits_raw = sb("logits_raw", [P, J, E])
        logits = sb("logits", [P, J, E])
        top = sb("top", [P, J, 8])
        top_at = sb("top_at", [P, J, 8], U32)
        at_f = sb("at_f", [P, J, 2])
        top_d = sb("top_d", [P, J, 8])
        top_e = sb("top_e", [P, J, 8])
        zsum = sb("zsum", [P, J, 1])
        rz = sb("rz", [P, J, 1])
        prob = sb("prob", [P, J, 2])
        psum2 = sb("psum2", [P, J, 1])
        rp = sb("rp", [P, J, 1])
        gate2 = sb("gate2", [P, J, 2])
        eq0, eq1, gate = [stats1[:].rearrange("p t s -> p (t s)")[:, i * J * E:(i + 1) * J * E].rearrange("p (j e) -> p j e", j=J)
                          for i in range(3)]

        C_ROW = bank("C_ROW")
        B_ROW = bank("B_ROW")
        SPARE = bank("SPARE")
        H1 = [bank(f"H1_{i}") for i in range(2)]
        H3 = [bank(f"H3_{i}") for i in range(2)]
        OUT = bank("OUT")

        ld_x = [sem(f"ld_x{q}") for q in range(PIECES)]
        ld_cst = sem("ld_cst")
        ld_adj = [sem(f"ld_adj{i}") for i in range(2)]
        ld_res = sem("ld_res")
        ld_w = sem("ld_w")
        ld_ffn = sem("ld_ffn")
        out_dma = sem("out_dma")
        pe_adj = sem("pe_adj")
        pe_g = sem("pe_g")
        pe_ht = sem("pe_ht")
        act_z = sem("act_z")
        pool_rg = sem("pool_rg")
        dve_hn = sem("dve_hn")
        pool_set = sem("pool_set")
        act_a = sem("act_a")
        dve_prep = sem("dve_prep")
        dve_mv1 = sem("dve_mv1")
        dve_mvg = sem("dve_mvg")
        pool_r1 = sem("pool_r1")
        dve_xn1 = sem("dve_xn1")
        dve_ffn_w = sem("dve_ffn_w")
        dve_c = sem("dve_c")
        dve_halved = sem("dve_halved")
        pool_own2 = sem("pool_own2")
        act_c = sem("act_c")
        pool_own1 = sem("pool_own1")
        pe_x = sem("pe_x")
        pe_z = sem("pe_z")
        spare_read = sem("spare_read")
        act_xth = sem("act_xth")
        act_zth = sem("act_zth")
        dve_u = sem("dve_u")
        pool_stack = sem("pool_stack")
        pool_sz = sem("pool_sz")
        pe_xp = sem("pe_xp")
        pe_dt = sem("pe_dt")
        act_ew = sem("act_ew")
        act_low = sem("act_low")
        act_ln = sem("act_ln")
        dve_dt = sem("dve_dt")
        dve_dtu = sem("dve_dtu")
        pe_B = sem("pe_B")
        pe_C = sem("pe_C")
        act_B = sem("act_B")
        act_keep = sem("act_keep")
        act_skip = sem("act_skip")
        dve_stack = sem("dve_stack")
        act_decay = sem("act_decay")
        pool_drive = sem("pool_drive")
        dve_scan = sem("dve_scan")
        dve_prod = sem("dve_prod")
        pool_y = sem("pool_y")
        dve_yg = sem("dve_yg")
        pe_wo = sem("pe_wo")
        own_n = sem("own_n")
        dve_mv2 = sem("dve_mv2")
        pool_r2 = sem("pool_r2")
        dve_xn2 = sem("dve_xn2")
        pe_xt = sem("pe_xt")
        act_now = sem("act_now")
        pe_rt = sem("pe_rt")
        dve_lg = sem("dve_lg")
        dve_td = sem("dve_td")
        act_te = sem("act_te")
        pe_gt = sem("pe_gt")
        dve_gate = sem("dve_gate")
        pool_gated = sem("pool_gated")
        pe_x2 = sem("pe_x2")
        pe_h1 = sem("pe_h1")
        pe_h3 = sem("pe_h3")
        act_th = sem("act_th")
        dve_a1 = sem("dve_a1")
        dve_hid = sem("dve_hid")
        pe_w2 = sem("pe_w2")
        act_out = sem("act_out")

        def over(ap, shape):
            return ap.broadcast_to(shape)

        small_loads = [
            (ident[:], A["identity"]), (iota[:], A["iota"].partition_broadcast(P)),
            (pick_f[:], A["pick"]),
            (gcn_w[:], A["gcn_w"]), (gcn_b[:], A["gcn_b"]),
            (ln_g[:], A["ln_g"]), (ln_b[:], A["ln_b"]),
            (conv_b[:], A["conv_b"]), (b_dt[:], A["b_dt"]), (d_skip[:], A["D_skip"]),
            (a_log[:], A["A_log"].rearrange("(h p) n -> p h n", p=P)),
        ]
        w_loads = [
            (w_in[:], A["w_in"]),
            (conv_wb[:], A["conv_w"].partition_broadcast(P)),
            (w_xp[:, :, 0:RANK], A["w_xp"].rearrange("(h p) m -> p h m", p=P)[:, :, 0:RANK]),
        ] + [
            (w_xp[:, :, BC0 + 32 * r:BC0 + 32 * r + 32],
             A["w_xp"].rearrange("(h p) m -> p h m", p=P)[:, :, RANK:RANK + 2 * NS]) for r in range(3)
        ] + [
            (w_dt[:], A["w_dt"]), (w_out[:], A["w_out"].rearrange("(h p) m -> p h m", p=P)),
            (router[:], A["router"]),
        ]
        ffn_loads = [
            (w1[:], A["w1"]), (w3[:], A["w3"]),
        ] + [(w2[0:M, m], A["w2"][m * P:m * P + M]) for m, M in enumerate(HT)]
        block = ctx.enter_context(nc.Block())

        @block.sync
        def _(sp):
            def load_x(q):
                rows = slice(q * PIECE, (q + 1) * PIECE)
                sp.dma_start(xn[:, rows, :], A["x"][:, rows, :]).then_inc(ld_x[q], 16)

            def load_piece(i):
                k, q = divmod(i, PIECES)
                if i >= 2:
                    sp.wait_ge(pe_adj, i - 1)
                sp.dma_start(adj_sb[:, i % 2], A["adj"][k, :, q * PIECE:(q + 1) * PIECE, :]).then_inc(ld_adj[i % 2], 16)

            def load_res(k):
                if not first(k):
                    sp.wait_ge(own_n, k)
                sp.dma_start(x_res[:], A["x"][:, bass.ds(k * J, J), :]).then_inc(ld_res, 16)

            def store(k):
                sp.wait_ge(act_out, k + 2)
                sp.dma_start(out[:, bass.ds(k * T, T)], out_sb[:]).then_inc(out_dma, 16)

            load_x(0)
            load_x(1)
            load_piece(0)
            load_x(2)
            load_x(3)
            load_piece(1)
            for dst, src in small_loads:
                sp.dma_start(dst, src).then_inc(ld_cst, 16)
            load_piece(2)
            load_piece(3)
            for dst, src in w_loads:
                sp.dma_start(dst, src).then_inc(ld_w, 16)
            for i in range(PIECES, 2 * PIECES + 2):
                load_piece(i)
            load_res(0)
            for dst, src in ffn_loads:
                sp.dma_start(dst, src).then_inc(ld_ffn, 16)
            for i in range(2 * PIECES + 2, CHUNKS * PIECES):
                load_piece(i)
            with sp.Fori(0, CHUNKS - 2) as c:
                load_res(c + 1)
                store(c)
            load_res(CHUNKS - 1)
            store(CHUNKS - 2)
            store(CHUNKS - 1)
            sp.wait_ge(out_dma, 16 * (CHUNKS + 1))

        @block.tensor
        def _(pe):
            head, loop, tail = program("pe")

            def piece(what, i, k, held):
                if what in SPARE_USERS and not (isinstance(held, int) and held == 0):
                    pe.wait_ge(spare_read, held)
                if what == "graph":
                    if i == 0 and not first(k):
                        pe.wait_ge(act_z, k)
                    if first(k):
                        pe.wait_ge(dve_xn1, i + 1)
                    pe.wait_ge(ld_adj[i % 2], 16 * ((k * PIECES + i) // 2 + 1))
                    for t in range(PIECE):
                        jt = i * PIECE + t
                        mm = pe.matmul(OUT[:], xn[:, jt, :], adj_sb[:, i % 2, t, :], start=(jt == 0), stop=(jt == JT - 1))
                    mm.then_inc(pe_adj, 1)
                elif what == "graph_g":
                    if first(k):
                        pe.wait_ge(ld_cst, 16 * len(small_loads))
                        pe.wait_ge(pool_set, 6)
                    pe.wait_ge(act_z, k + 1)
                    for j in range(J):
                        pe.matmul(SPARE[:, j * P:(j + 1) * P], z_sb[:, j * P:(j + 1) * P], gcn_w[:], start=True, stop=False)
                        mm = pe.matmul(SPARE[:, j * P:(j + 1) * P], ones_row[:], gcn_b[:], start=False, stop=True)
                    mm.then_inc(pe_g, 1)
                elif what == "graph_turn":
                    pe.wait_ge(dve_hn, k + 1)
                    for j in range(J):
                        mm = pe.transpose(SPARE[:, j * P:(j + 1) * P], h_nrm[:, j, :], ident[:])
                    mm.then_inc(pe_ht, 1)
                elif what == "x":
                    if first(k) and i == 0:
                        pe.wait_ge(ld_w, 16 * len(w_loads))
                        pe.wait_ge(dve_prep, 1)
                    for tap in range(TAPS):
                        mm = pe.matmul(SPARE[:], w_tap[:, tap, i * P:(i + 1) * P], h_t[:, bass.ds(k * T + tap, T)],
                                       start=(tap == 0), stop=(tap == TAPS - 1))
                    mm.then_inc(pe_x, 1)
                elif what == "z":
                    pe.wait_ge(dve_u, k + 1)
                    pe.matmul(SPARE[:], w_in[:, DI + i * P:DI + (i + 1) * P], h_t[:, bass.ds(k * T + PRE, T)],
                              start=True, stop=True).then_inc(pe_z, 1)
                elif what == "xp":
                    pe.wait_ge(dve_u, k + 1)
                    for h in range(HALVES):
                        mm = pe.matmul(SPARE[:], w_xp[:, h, :], u[:, h, :], start=(h == 0), stop=(h == HALVES - 1))
                    mm.then_inc(pe_xp, 1)
                elif what == "dt":
                    pe.matmul(SPARE[:], w_dt[:, i * P:(i + 1) * P], xps[0:RANK, :], start=True, stop=True).then_inc(pe_dt, 1)
                elif what == "row_b":
                    if i == 0:
                        pe.wait_ge(dve_stack, k + 1)
                    if not first(k) or i >= 1:
                        pe.wait_ge(act_B, k * NS + i)
                    pe.matmul(B_ROW[:], over(pick[:, i:i + 1], [P, P]), stack[:], start=True, stop=True).then_inc(pe_B, 1)
                elif what == "row_c":
                    if i == 0:
                        pe.wait_ge(dve_stack, k + 1)
                    if not first(k) or i >= 1:
                        pe.wait_ge(dve_prod, k * NS + i)
                    pe.matmul(C_ROW[:], over(pick[:, NS + i:NS + i + 1], [P, P]), stack[:], start=True, stop=True).then_inc(pe_C, 1)
                elif what == "w_out":
                    pe.wait_ge(dve_yg, k + 1)
                    for j in range(J):
                        for h in range(HALVES):
                            mm = pe.matmul(SPARE[:, j * P:(j + 1) * P], yg[:, h, j * P:(j + 1) * P], w_out[:, h, :],
                                           start=(h == 0), stop=(h == HALVES - 1))
                    mm.then_inc(pe_wo, 1)
                elif what == "x_turn":
                    pe.wait_ge(dve_xn2, k + 1)
                    for j in range(J):
                        mm = pe.transpose(SPARE[:, j * P:(j + 1) * P], xn2[:, j, :], ident[:])
                    mm.then_inc(pe_xt, 1)
                elif what == "route":
                    pe.wait_ge(act_now, k + 1)
                    for j in range(J):
                        mm = pe.matmul(SPARE[:, j * E:(j + 1) * E], x_now[:, j * P:(j + 1) * P], router[:], start=True, stop=True)
                    mm.then_inc(pe_rt, 1)
                elif what == "gate_x":
                    pe.wait_ge(pool_gated, k * E + i + 1)
                    for j in range(J):
                        mm = pe.transpose(SPARE[:, j * P:(j + 1) * P], gated[:, i % 2, j, :], ident[:])
                    mm.then_inc(pe_gt, 1)
                elif what == "ffn_open":
                    pe.wait_ge(act_out, k + 1)
                    pe.wait_ge(act_z, CHUNKS)
                    pe.wait_ge(dve_gate, k + 1)
                    for j in range(J):
                        mm = pe.matmul(OUT[:, j * P:(j + 1) * P], x2[:, j, :], ident[:], start=(j == 0), stop=False,
                                       skip_group_check=True)
                    mm.then_inc(pe_x2, 1)
                elif what == "step":
                    e, m = divmod(i, len(HT))
                    M = HT[m]
                    col = e * HID + m * P
                    if i >= 2:
                        pe.wait_ge(dve_a1, k * STEPS + i - 1)
                    pe.matmul(H1[i % 2][0:M, :], w1[:, col:col + M], x_t(k), start=True, stop=True).then_inc(pe_h1, 1)
                    if m == 0:
                        pe.wait_ge(spare_read, held)
                    if i >= 2:
                        pe.wait_ge(dve_hid, k * STEPS + i - 1)
                    pe.matmul(H3[i % 2][0:M, :], w3[:, col:col + M], gx[:, e % 4, :], start=True, stop=True).then_inc(pe_h3, 1)
                    if i >= 2:
                        down(i - 2, k)
                elif what == "ffn_close":
                    down(STEPS - 2, k)
                    down(STEPS - 1, k)

            def down(i, c):
                e, m = divmod(i, len(HT))
                pe.wait_ge(dve_hid, c * STEPS + i + 1)
                pe.matmul(OUT[:], w2[0:HT[m], m, e, :], hid[0:HT[m], i % 3, :], start=False, stop=(i == STEPS - 1),
                          skip_group_check=True).then_inc(pe_w2, 1)

            for p in head:
                piece(*p)
            pe.wait_ge(ld_ffn, 16 * len(ffn_loads))
            pe.wait_ge(dve_ffn_w, 1)
            with pe.Fori(0, CHUNKS - 2) as c:
                for p in loop(c):
                    piece(*p)
            for p in tail:
                piece(*p)

        @block.scalar
        def _(act):
            head, loop, tail = program("act")

            def piece(what, i, k, held):
                if what == "graph_z":
                    act.wait_ge(pe_adj, PIECES * (k + 1))
                    if not first(k):
                        act.wait_ge(pe_g, k)
                    act.copy(z_sb[:], OUT[:]).then_inc(act_z, 1)
                elif what == "graph_g":
                    act.wait_ge(pe_g, k + 1)
                    if not first(k):
                        act.wait_ge(pe_ht, k)
                    act.activation(g_act[:], SPARE[:].rearrange("p (j c) -> p j c", j=J), ACT.Relu).then_inc(spare_read, 1)
                elif what == "graph_turn":
                    act.wait_ge(pe_ht, k + 1)
                    act.activation(h_t[:, bass.ds(PRE + k * T, T)], SPARE[:], ACT.Identity, scale=ln_g[:], bias=ln_b[:])\
                       .then_inc(spare_read, 1)
                elif what == "x":
                    if first(k):
                        act.wait_ge(dve_prep, 1)
                    act.wait_ge(pe_x, 2 * k + i + 1)
                    if i == 0 and not first(k):
                        act.wait_ge(dve_dt, k)
                    act.activation(xh[:, i, :], SPARE[:], ACT.Identity, bias=conv_bh[:, i:i + 1]).then_inc(spare_read, 1)
                elif what == "u":
                    act.wait_ge(spare_read, held)
                    act.activation(xth[:], xh[:], ACT.Tanh).then_inc(act_xth, 1)
                elif what == "z":
                    act.wait_ge(pe_z, 2 * k + i + 1)
                    if i == 0:
                        act.wait_ge(dve_dt, k + 1)
                    act.copy(zh[:, i, :], SPARE[:]).then_inc(spare_read, 1)
                    if i == HALVES - 1:
                        act.wait_ge(spare_read, held + 1)
                        act.activation(zth[:], zh[:], ACT.Tanh).then_inc(act_zth, 1)
                elif what == "xp":
                    act.wait_ge(pe_xp, k + 1)
                    if not first(k):
                        act.wait_ge(pool_stack, k)
                    act.copy(xps[:], SPARE[:]).then_inc(spare_read, 1)
                elif what == "dt":
                    if i == 0 and not first(k):
                        act.wait_ge(pool_sz, k)
                    act.wait_ge(pe_dt, 2 * k + i + 1)
                    act.activation(pre[:, i, :], SPARE[:], ACT.Identity, bias=b_dt[:, i:i + 1]).then_inc(spare_read, 1)
                    if i == HALVES - 1:
                        act.wait_ge(spare_read, held + 1)
                        act.activation(ab[:], pre[:], ACT.Abs).then_inc(act_c, 1)
                        act.wait_ge(act_c, k + 1)
                        act.activation(ew[:], ab[:], ACT.Exp, scale=-1.0).then_inc(act_ew, 1)
                        act.wait_ge(act_ew, k + 1)
                        act.wait_ge(pool_stack, k + 1)
                        act.activation(low[:], ew[:], ACT.Identity, bias=1.0).then_inc(act_low, 1)
                        act.wait_ge(act_low, k + 1)
                        act.activation(ln1p[:], low[:], ACT.Ln).then_inc(act_ln, 1)
                elif what == "decay":
                    if i == 0:
                        act.wait_ge(dve_dt, k + 1)
                    if not first(k) or i >= 2:
                        act.wait_ge(dve_scan, 2 * (k * NS + i - 1))
                    for h in range(HALVES):
                        act.activation(decay[:, i % 2, h, :], dt_[:, h, :], ACT.Exp, scale=a_neg[:, h, i:i + 1]).then_inc(act_decay, 1)
                elif what == "row_b":
                    act.wait_ge(pe_B, k * NS + i + 1)
                    if not first(k) or i >= 2:
                        act.wait_ge(pool_drive, k * NS + i - 1)
                    act.copy(b_row[:, i % 2, :], B_ROW[:]).then_inc(act_B, 1)
                elif what == "keep":
                    act.wait_ge(dve_scan, 2 * (k * NS + i + 1))
                    act.copy(state[:, i, :], hs[:, i % 2, :, T - 1]).then_inc(act_keep, 1)
                elif what == "skip":
                    act.wait_ge(dve_u, k + 1)
                    if not first(k):
                        act.wait_ge(dve_yg, k)
                    for h in range(HALVES):
                        act.activation(yown[:, h, :], u[:, h, :], ACT.Identity, scale=d_skip[:, h:h + 1]).then_inc(act_skip, 1)
                elif what == "x_turn":
                    act.wait_ge(pe_xt, k + 1)
                    act.copy(x_now[:], SPARE[:]).then_inc(act_now, 1)
                    act.copy(x_t(k), SPARE[:]).then_inc(spare_read, 1)
                elif what == "route":
                    act.wait_ge(pe_rt, k + 1)
                    act.copy(logits_raw[:], SPARE[:, 0:J * E].rearrange("p (j e) -> p j e", j=J)).then_inc(spare_read, 1)
                elif what == "top_exp":
                    act.wait_ge(dve_td, k + 1)
                    act.activation(top_e[:], top_d[:], ACT.Exp).then_inc(act_te, 1)
                elif what == "gate_x":
                    act.wait_ge(pe_gt, k * E + i + 1)
                    if i >= 4:
                        act.wait_ge(pe_h3, k * STEPS + len(HT) * (i - 3))
                    act.copy(gx[:, i % 4, :], SPARE[:]).then_inc(spare_read, 1)
                elif what == "step":
                    M = HT[i % len(HT)]
                    act.wait_ge(pe_h1, k * STEPS + i + 1)
                    if i >= 4:
                        act.wait_ge(dve_hid, k * STEPS + i - 3)
                    act.activation(th[0:M, i % 4, :], H1[i % 2][0:M, :], ACT.Tanh).then_inc(act_th, 1)
                elif what == "ffn_out":
                    act.wait_ge(pe_w2, (k + 1) * STEPS)
                    act.wait_ge(out_dma, 16 * (k + 1))
                    act.copy(out_sb[:], OUT[:]).then_inc(act_out, 1)

            act.wait_ge(ld_cst, 16 * len(small_loads))
            act.activation(a_exp[:], a_log[:], ACT.Exp).then_inc(act_a, 1)
            for p in head:
                piece(*p)
            with act.Fori(0, CHUNKS - 2) as c:
                for p in loop(c):
                    piece(*p)
            for p in tail:
                piece(*p)

        @block.vector
        def _(dve):
            head, loop, tail = program("dve")

            def row_stats(rows, stats, mv, own_stats, k, done):
                for j in range(J):
                    bn = dve.bn_stats(stats[:, j, :], rows[:, j, :])
                bn.then_inc(own_stats, 1)
                for j in range(J):
                    dve.wait_ge(ld_x[0], 16)
                    dve.wait_ge(own_stats, k + 1)
                    bn = dve.bn_aggr(mv[:, j, :], stats[:, j, :])
                bn.then_inc(done, 1)

            def norm_rows(dst, rows, mv, rs, tiles, done):
                for j in range(tiles):
                    last = dve.tensor_scalar(dst[:, j, :], rows[:, j, :], mv[:, j, 0:1], rs[:, j:j + 1], ALU.subtract, ALU.mult)
                last.then_inc(done, 1)

            def piece(what, i, k, held):
                if what == "graph_rows":
                    dve.wait_ge(spare_read, held)
                    row_stats(g_act, statsg, mvg, own_gs, k, dve_mvg)
                elif what == "graph_norm":
                    dve.wait_ge(pool_rg, k + 1)
                    norm_rows(h_nrm, g_act, mvg, rsg, J, dve_hn)
                elif what == "u":
                    dve.wait_ge(act_xth, k + 1)
                    if not first(k):
                        dve.wait_ge(act_skip, 2 * k)
                    dve.scalar_tensor_tensor(u[:], xth[:], 1.0, xh[:], ALU.add, ALU.mult).then_inc(dve_u, 1)
                elif what == "soft":
                    if i == 0:
                        dve.wait_ge(act_ln, k + 1)
                        ins = dve.scalar_tensor_tensor(low[:], low[:], 1.0, ew[:], ALU.subtract, ALU.subtract)
                    else:
                        dve.wait_ge(own_s, 2 * k + 1)
                        ins = dve.tensor_tensor(low[:], ln1p[:], low[:], ALU.subtract)
                    ins.then_inc(own_s, 1)
                elif what == "turn_over":
                    dve.wait_ge(own_s, 2 * k + 2)
                    if not first(k):
                        dve.wait_ge(act_decay, 2 * k * NS)
                    dve.scalar_tensor_tensor(dt_[:], pre[:], 0.0, low[:], ALU.max, ALU.add).then_inc(dve_dt, 1)
                    if not first(k):
                        dve.wait_ge(pe_C, k * NS)
                    dve.tensor_copy(stack[:], stack_next[:]).then_inc(dve_stack, 1)
                    dve.wait_ge(dve_dt, k + 1)
                    if not first(k):
                        dve.wait_ge(pool_drive, k * NS)
                    dve.tensor_tensor(dtu[:], dt_[:], u[:], ALU.mult).then_inc(dve_dtu, 1)
                elif what == "weigh":
                    weigh(i, k)
                elif what == "scan":
                    if i == NS - 1:
                        own_add(NS - 2, k)
                        dve.wait_ge(pool_y, adds_before(k + 1))
                        dve.wait_ge(own_y, own_before(k + 1) - 2)
                        dve.tensor_tensor(yown[:], yown[:], yacc[:], ALU.add).then_inc(own_y, 1)
                    dve.wait_ge(pool_drive, k * NS + i + 1)
                    for h in range(HALVES):
                        dve.wait_ge(act_decay, 2 * (k * NS + i) + h + 1)
                        start = 0.0 if first(k) else state[:, i, h:h + 1]
                        if h == 0 and (not first(k) or i >= 2):
                            dve.wait_ge(act_keep, k * NS + i - 1)
                            dve.wait_ge(dve_prod, k * NS + i - 1)
                        dve.tensor_tensor_scan(hs[:, i % 2, h, :], decay[:, i % 2, h, :], drive[:, i % 2, h, :], start,
                                               ALU.mult, ALU.add).then_inc(dve_scan, 1)
                elif what == "gate_y":
                    own_add(NS - 1, k)
                    dve.wait_ge(own_y, own_before(k + 1))
                    dve.wait_ge(pool_sz, k + 1)
                    dve.tensor_tensor(yg[:], yown[:], sz[:], ALU.mult).then_inc(dve_yg, 1)
                elif what == "norm":
                    dve.wait_ge(pe_wo, k + 1)
                    if not first(k):
                        dve.wait_ge(pe_x2, k)
                    dve.wait_ge(ld_res, 16 * (k + 1))
                    dve.tensor_tensor(x2[:], SPARE[:].rearrange("p (j c) -> p j c", j=J),
                                      x_res[:], ALU.add).then_inc(spare_read, 1)
                    dve.wait_ge(spare_read, held)
                    row_stats(x2, stats2, mv2, own_n, k, dve_mv2)
                elif what == "x_turn":
                    dve.wait_ge(pool_r2, k + 1)
                    if not isinstance(k, int) or k > 0:
                        dve.wait_ge(pool_gated, k * E)
                    norm_rows(xn2, x2, mv2, rs2, J, dve_xn2)
                elif what == "route":
                    route(k, held)
                elif what == "step":
                    M = HT[i % len(HT)]
                    dve.wait_ge(act_th, k * STEPS + i + 1)
                    dve.scalar_tensor_tensor(th[0:M, i % 4, :], th[0:M, i % 4, :], 1.0, H1[i % 2][0:M, :], ALU.add, ALU.mult)\
                       .then_inc(dve_a1, 1)
                    if i >= 1:
                        hidden(i - 1, k)
                elif what == "ffn_close":
                    hidden(STEPS - 1, k)

            def hidden(i, k):
                M = HT[i % len(HT)]
                dve.wait_ge(dve_a1, k * STEPS + i + 1)
                dve.wait_ge(pe_h3, k * STEPS + i + 1)
                if i >= 3:
                    dve.wait_ge(pe_w2, k * STEPS + i - 2)
                dve.tensor_tensor(hid[0:M, i % 3, :], th[0:M, i % 4, :], H3[i % 2][0:M, :], ALU.mult).then_inc(dve_hid, 1)

            def weigh(i, k):
                own = own_states(k)
                c_row = over(C_ROW[:].unsqueeze(1), [P, HALVES, T])
                if i - 1 in own and i - 1 != NS - 2:
                    own_add(i - 1, k)
                dve.wait_ge(pe_C, k * NS + i + 1)
                dve.wait_ge(dve_scan, 2 * (k * NS + i + 1))
                if i in own:
                    if own.index(i) >= 1 or not first(k):
                        dve.wait_ge(own_y, own_before(k) + own.index(i) + (i == NS - 1))
                    dst = ptmp[:]
                else:
                    nth = [n for n in range(NS) if n not in own].index(i)
                    if nth == 0:
                        if not first(k):
                            dve.wait_ge(pe_wo, k)
                        dst = yacc[:]
                    else:
                        dst = prod[:, nth % 2]
                        if nth >= 3:
                            dve.wait_ge(pool_y, adds_before(k) + nth - 2)
                dve.tensor_tensor(dst, hs[:, i % 2], c_row, ALU.mult).then_inc(dve_prod, 1)

            def own_add(i, k):
                own = own_states(k)
                nth = own.index(i)
                dve.wait_ge(dve_prod, k * NS + i + 1)
                if nth == 0:
                    dve.wait_ge(act_skip, 2 * (k + 1))
                else:
                    dve.wait_ge(own_y, own_before(k) + nth + (i == NS - 1))
                dve.tensor_tensor(yown[:], yown[:], ptmp[:], ALU.add).then_inc(own_y, 1)

            def route(k, held):
                n = [0]

                def own(ins):
                    n[0] += 1
                    ins.then_inc(own_r, 1)
                    dve.wait_ge(own_r, ROUTE * k + n[0])

                dve.wait_ge(spare_read, held + 1)
                dve.tensor_copy(logits[:], logits_raw[:]).then_inc(dve_lg, 1)
                for j in range(J):
                    dve.wait_ge(ld_x[0], 16)
                    dve.wait_ge(dve_lg, k + 1)
                    dve.max(top[:, j, :], logits[:, j, :]).then_inc(own_r, 1)
                dve.wait_ge(own_r, ROUTE * k + J)
                dve.tensor_tensor(top_d[:], top[:], over(top[:, :, 0:1], [P, J, 8]), ALU.subtract).then_inc(dve_td, 1)
                for j in range(J):
                    dve.max_index(top_at[:, j, :], top[:, j, :], logits[:, j, :]).then_inc(own_r, 1)
                n[0] = 2 * J
                dve.wait_ge(own_r, ROUTE * k + 2 * J)
                own(dve.tensor_copy(at_f[:], top_at[:, :, 0:2]))
                own(dve.tensor_tensor(eq0, over(iota[:].unsqueeze(1), [P, J, E]), over(at_f[:, :, 0:1], [P, J, E]), ALU.is_equal))
                own(dve.tensor_tensor(eq1, over(iota[:].unsqueeze(1), [P, J, E]), over(at_f[:, :, 1:2], [P, J, E]), ALU.is_equal))
                dve.wait_ge(act_te, k + 1)
                own(dve.tensor_reduce(zsum[:], top_e[:], mybir.AxisListType.X, ALU.add))
                own(dve.reciprocal(rz[:], zsum[:]))
                own(dve.tensor_tensor(prob[:], top_e[:, :, 0:2], over(rz[:], [P, J, 2]), ALU.mult))
                own(dve.tensor_tensor(psum2[:], prob[:, :, 0:1], prob[:, :, 1:2], ALU.add))
                own(dve.tensor_scalar(psum2[:], psum2[:], 1e-9, None, ALU.add))
                own(dve.reciprocal(rp[:], psum2[:]))
                own(dve.tensor_tensor(gate2[:], prob[:], over(rp[:], [P, J, 2]), ALU.mult))
                own(dve.tensor_tensor(eq0, eq0, over(gate2[:, :, 0:1], [P, J, E]), ALU.mult))
                own(dve.tensor_tensor(eq1, eq1, over(gate2[:, :, 1:2], [P, J, E]), ALU.mult))
                dve.tensor_tensor(gate, eq0, eq1, ALU.add).then_inc(dve_gate, 1)
                assert n[0] == ROUTE

            own_s, own_y, own_r, own_gs = [sem(n) for n in ("own_s", "own_y", "own_r", "own_gs")]
            ROUTE = 20

            for q in range(PIECES + 1):
                if q < PIECES:
                    rows = range(q * PIECE, (q + 1) * PIECE)
                    dve.wait_ge(ld_x[q], 16)
                    for j in rows:
                        dve.bn_stats(stats1[:, j, :], xn[:, j, :]).then_inc(dve_c, 1)
                    for j in rows:
                        dve.wait_ge(dve_c, j + 1)
                        bn = dve.bn_aggr(mv1[:, j, :], stats1[:, j, :])
                    bn.then_inc(dve_mv1, 1)
                if q >= 1:
                    rows = slice((q - 1) * PIECE, q * PIECE)
                    dve.wait_ge(pool_r1, q)
                    norm_rows(xn[:, rows], xn[:, rows], mv1[:, rows], rs1[:, rows], PIECE, dve_xn1)
            dve.wait_ge(ld_cst, 16 * len(small_loads))
            dve.wait_ge(act_a, 1)
            dve.tensor_scalar(a_neg[:], a_exp[:], -1.0, None, ALU.mult).then_inc(dve_c, 1)
            dve.tensor_scalar(conv_bh[:], conv_b[:], 0.5, None, ALU.mult).then_inc(dve_c, 1)
            dve.wait_ge(ld_w, 16 * len(w_loads))
            dve.scalar_tensor_tensor(w_tap[:], conv_wb[:], 0.5, over(w_in[:, 0:DI].unsqueeze(1), [P, TAPS, DI]), ALU.mult, ALU.mult)\
               .then_inc(dve_c, 1)
            dve.tensor_scalar(w_in[:, DI:2 * DI], w_in[:, DI:2 * DI], 0.5, None, ALU.mult).then_inc(dve_halved, 1)
            dve.wait_ge(dve_c, JT + 3)
            dve.wait_ge(dve_halved, 1)
            dve.wait_ge(pool_set, 7)
            dve.engine_nop().then_inc(dve_prep, 1)
            for p in head:
                piece(*p)
            dve.wait_ge(ld_ffn, 16 * len(ffn_loads))
            dve.tensor_scalar(w1[:], w1[:], 0.5, None, ALU.mult).then_inc(dve_ffn_w, 1)
            with dve.Fori(0, CHUNKS - 2) as c:
                for p in loop(c):
                    piece(*p)
            for p in tail:
                piece(*p)

        @block.gpsimd
        def _(pool):
            head, loop, tail = program("pool")

            def rstd(mv, ve, rs, n, own, at, done):
                pool.tensor_tensor(ve[:, :], mv[:, :, 1], eps_row[:, 0:n], ALU.add).then_inc(own, 1)
                pool.wait_ge(own, at + 1)
                pool.tensor_tensor(rs[:, :], ve[:, :], minus_half[:, 0:n], ALU.pow).then_inc(done, 1)

            def piece(what, i, k, held):
                if what == "graph_rows":
                    pool.wait_ge(dve_mvg, k + 1)
                    rstd(mvg, veg, rsg, J, own_g, k, pool_rg)
                elif what == "z":
                    if i < HALVES - 1:
                        return
                    pool.wait_ge(act_zth, k + 1)
                    if not first(k):
                        pool.wait_ge(dve_yg, k)
                    pool.tensor_tensor(zth[:], zth[:], over(one[:].unsqueeze(2), [P, HALVES, T]), ALU.add).then_inc(own_z, 1)
                    pool.wait_ge(own_z, k + 1)
                    pool.tensor_tensor(sz[:], zth[:], zh[:], ALU.mult).then_inc(pool_sz, 1)
                elif what == "xp":
                    pool.wait_ge(spare_read, held + 1)
                    if not first(k):
                        pool.wait_ge(dve_stack, k)
                    at = 4 * k
                    pool.tensor_tensor(stack_next[:], xps[:], over(one[:, 0:1], [P, T]), ALU.mult).then_inc(own_b, 1)
                    pool.wait_ge(own_b, at + 1)
                    pool.tensor_tensor(rest[64:128, :], xps[64:128, :], stack_next[64:128, :], ALU.subtract).then_inc(own_b, 1)
                    pool.wait_ge(own_b, at + 2)
                    pool.tensor_tensor(stack_next[64:128, :], rest[64:128, :], over(one[64:128, 0:1], [64, T]), ALU.mult).then_inc(own_b, 1)
                    pool.wait_ge(own_b, at + 3)
                    pool.tensor_tensor(rest[96:128, :], rest[96:128, :], stack_next[96:128, :], ALU.subtract).then_inc(own_b, 1)
                    pool.wait_ge(own_b, at + 4)
                    pool.tensor_tensor(stack_next[96:128, :], rest[96:128, :], over(one[96:128, 0:1], [32, T]), ALU.mult)\
                        .then_inc(pool_stack, 1)
                    pool.wait_ge(pool_stack, k + 1)
                elif what == "drive":
                    if i == 0:
                        pool.wait_ge(dve_dtu, k + 1)
                    pool.wait_ge(act_B, k * NS + i + 1)
                    if not first(k) or i >= 2:
                        pool.wait_ge(dve_scan, 2 * (k * NS + i - 1))
                    pool.tensor_tensor(drive[:, i % 2], dtu[:], over(b_row[:, i % 2, :].unsqueeze(1), [P, HALVES, T]), ALU.mult)\
                        .then_inc(pool_drive, 1)
                elif what == "add":
                    add(i, k)
                elif what == "norm":
                    pool.wait_ge(dve_mv2, k + 1)
                    rstd(mv2, ve2, rs2, J, pool_own2, k, pool_r2)
                elif what == "gated":
                    if i == 0:
                        pool.wait_ge(dve_gate, k + 1)
                    if i >= 2:
                        pool.wait_ge(pe_gt, k * E + i - 1)
                    pool.tensor_tensor(gated[:, i % 2], xn2[:], over(gate[:, :, i:i + 1], [P, J, D]), ALU.mult)\
                        .then_inc(pool_gated, 1)

            def add(i, k):
                ours = [n for n in range(NS) if n not in own_states(k)]
                if i not in ours[1:]:
                    return
                nth = ours.index(i)
                pool.wait_ge(dve_prod, k * NS + i + 1)
                if nth >= 2:
                    pool.wait_ge(pool_y, adds_before(k) + nth - 1)
                pool.tensor_tensor(yacc[:], yacc[:], prod[:, nth % 2], ALU.add).then_inc(pool_y, 1)

            own_z, own_b, own_g = sem("own_z"), sem("own_b"), sem("own_g")
            pool.memset(out_sb[:, 1:2], 0.0).then_inc(act_out, 1)
            pool.memset(out_sb[:, 0:1], 0.0).then_inc(out_dma, 16)
            pool.memset(minus_half[:], -0.5).then_inc(pool_set, 1)
            pool.memset(w_xp[:, :, RANK:BC0], 0.0).then_inc(pool_set, 1)
            pool.memset(h_t[:, 0:PRE], 0.0).then_inc(pool_set, 1)
            pool.memset(eps_row[:], EPS).then_inc(pool_set, 1)
            pool.memset(one[:], 1.0).then_inc(pool_set, 1)
            pool.memset(ones_row[:], 1.0).then_inc(pool_set, 1)
            pool.wait_ge(pool_set, 6)
            for q in range(PIECES):
                pool.wait_ge(dve_mv1, q + 1)
                rows = slice(q * PIECE, (q + 1) * PIECE)
                rstd(mv1[:, rows], ve1[:, rows], rs1[:, rows], PIECE, pool_own1, q, pool_r1)
            pool.wait_ge(ld_cst, 16 * len(small_loads))
            pool.tensor_copy(pick[:], pick_f[:]).then_inc(pool_set, 1)
            for p in head:
                piece(*p)
            with pool.Fori(0, CHUNKS - 2) as c:
                for p in loop(c):
                    piece(*p)
            for p in tail:
                piece(*p)


def kernel(x, adj, L0_gnn_gcn_w, L0_gnn_gcn_b, L0_gnn_ln_g, L0_gnn_ln_b, L0_gnn_w_in, L0_gnn_conv_w,
           L0_gnn_conv_b, L0_gnn_w_xp, L0_gnn_w_dt, L0_gnn_b_dt, L0_gnn_A_log, L0_gnn_D_skip, L0_gnn_w_out,
           L0_ffn_router_w, L0_ffn_w1, L0_ffn_w2, L0_ffn_w3):
    import numpy as np
    import concourse.bacc as bacc
    from concourse.bass_utils import run_bass_kernel_spmd

    def tiles(a):
        a = np.asarray(a)
        return a.reshape(-1, P, a.shape[1]).transpose(1, 0, 2)

    def channels(v):
        return np.asarray(v).reshape(HALVES, P).T

    pick = np.zeros((P, 2 * NS), np.float32)
    for r in range(3):
        pick[BC0 + 32 * r:BC0 + 32 * r + 32, :] = np.eye(2 * NS, dtype=np.float32)
    arrays = {
        "x": tiles(x),
        "adj": np.asarray(adj).reshape(CHUNKS, T, JT, P).transpose(0, 3, 2, 1),
        "gcn_w": L0_gnn_gcn_w, "gcn_b": np.asarray(L0_gnn_gcn_b).reshape(1, D),
        "ln_g": np.asarray(L0_gnn_ln_g).reshape(D, 1), "ln_b": np.asarray(L0_gnn_ln_b).reshape(D, 1),
        "w_in": L0_gnn_w_in, "conv_w": np.asarray(L0_gnn_conv_w).T, "conv_b": channels(L0_gnn_conv_b),
        "w_xp": L0_gnn_w_xp, "w_dt": L0_gnn_w_dt, "b_dt": channels(L0_gnn_b_dt),
        "A_log": L0_gnn_A_log, "D_skip": channels(L0_gnn_D_skip), "w_out": L0_gnn_w_out,
        "router": np.asarray(L0_ffn_router_w).T,
        "w1": np.asarray(L0_ffn_w1).reshape(E * HID, D).T,
        "w3": np.asarray(L0_ffn_w3).reshape(E * HID, D).T,
        "w2": np.asarray(L0_ffn_w2).transpose(2, 0, 1),
        "identity": np.eye(P, dtype=np.float32),
        "pick": pick,
        "iota": np.arange(E, dtype=np.float32),
    }
    nc = bacc.Bacc("TRN2", target_bir_lowering=False, num_devices=1)
    sent, args = {}, {}
    for name, a in arrays.items():
        a = np.ascontiguousarray(a)
        sent[f"in_{name}"] = a
        args[name] = nc.dram_tensor(f"in_{name}", a.shape, mybir.dt.from_np(a.dtype), kind="ExternalInput").ap()
    out = nc.dram_tensor("out_t", (D, L), F32, kind="ExternalOutput").ap()
    build_kernel(nc, args, out)
    result = run_bass_kernel_spmd(nc, [sent], core_ids=[0])
    return np.ascontiguousarray(result.results[0]["out_t"].T)
```
